# Optimizing a Trainium2 kernel written in Bass

```python
import numpy as np
import jax
import jax.numpy as jnp

def _softmax(x, axis=-1):
    return jax.nn.softmax(x, axis=axis)

def _gelu(x):
    return jax.nn.gelu(x, approximate=True)

def _silu(x):
    return jax.nn.silu(x)

def _sigmoid(x):
    return jax.nn.sigmoid(x)

def _layernorm(x, axis=-1, eps=1e-05):
    m = jnp.mean(x, axis=axis, keepdims=True)
    v = jnp.var(x, axis=axis, keepdims=True)
    return (x - m) / jnp.sqrt(v + eps)

def _scatter_add(tgt, idx, src, axis=0):
    return tgt.at[idx].add(src)

def _segment_sum(src, seg, n):
    return jax.ops.segment_sum(src, seg, n)
kernel_name = 'mk_vit_tower_postln_d1_tok_img768_r4_d856a1'

def setup_inputs(seed: int=0):
    np.random.seed(seed)
    _w = jnp.asarray

    def _rec_inputs():
        import jax
        import jax.numpy as jnp
        _rk = jax.random.key(seed)
        x = 7.57192e-06 + 1.00007 * jax.random.normal(jax.random.fold_in(_rk, 1), (16, 3, 96, 96), jnp.float32)
        return x
    x = _rec_inputs()

    def _L0_tok_setup():
        import jax, jax.numpy as jnp
        import numpy as np
        B, IN, IMG = (64, 3, 224)
        PATCH, LEVELS, D = (16, 4, 192)
        ISQ2 = 0.7071067811865476
        DN = ('NCHW', 'OIHW', 'NCHW')

        def conv(x, w, b=None, stride=1, pad=((0, 0), (0, 0)), groups=1):
            y = jax.lax.conv_general_dilated(x, w, (stride, stride), pad, dimension_numbers=DN, feature_group_count=groups)
            return y if b is None else y + b[None, :, None, None]

        def dwconv(x, wd, wp, bp):
            y = conv(x, wd, pad=((1, 1), (1, 1)), groups=x.shape[1])
            return conv(y, wp, bp)

        def haar_dwt2(x):
            xe, xo = (x[..., ::2], x[..., 1::2])
            lo_w, hi_w = ((xe + xo) * ISQ2, (xe - xo) * ISQ2)

            def split_h(t):
                te, to = (t[..., ::2, :], t[..., 1::2, :])
                return ((te + to) * ISQ2, (te - to) * ISQ2)
            ll, lh = split_h(lo_w)
            hl, hh = split_h(hi_w)
            return (ll, lh, hl, hh)

        def wavelet_packet(x):
            f = x
            for _ in range(LEVELS):
                b, k, h, w = f.shape
                ll, lh, hl, hh = haar_dwt2(f)
                bands = jnp.stack([ll, lh, hl, hh], axis=1)
                bands = bands.reshape(b, 4, k // IN, IN, h // 2, w // 2)
                f = jnp.transpose(bands, (0, 2, 1, 3, 4, 5)).reshape(b, 4 * k, h // 2, w // 2)
            return f

        def gelu(x):
            return jax.nn.gelu(x, approximate=False)

        def forward(x, pl_w, pl_b, pl_dw, pl_pw, pl_pwb, pg_w1, pg_b1, pg_dw, pg_pw, pg_pwb, pg_w2, pg_b2, alpha, f1_dw, f1_pw, f1_pwb, f2_dw, f2_pw, f2_pwb, f3_dw, f3_pw, f3_pwb, ln_g, ln_b, cls):
            loc = conv(x, pl_w, pl_b, stride=PATCH)
            loc = dwconv(gelu(loc), pl_dw, pl_pw, pl_pwb)
            g = wavelet_packet(x)
            g = gelu(conv(g, pg_w1, pg_b1))
            g = gelu(dwconv(g, pg_dw, pg_pw, pg_pwb))
            glob = conv(g, pg_w2, pg_b2)
            gate = 0.5 * (jnp.tanh(alpha) + 1.0)
            h = (1.0 - gate) * loc + gate * glob
            h = jax.nn.relu(dwconv(h, f1_dw, f1_pw, f1_pwb))
            h = jax.nn.relu(dwconv(h, f2_dw, f2_pw, f2_pwb))
            h = dwconv(loc + h, f3_dw, f3_pw, f3_pwb)
            t = jnp.transpose(h.reshape(h.shape[0], D, -1), (0, 2, 1))
            mu = jnp.mean(t, -1, keepdims=True)
            var = jnp.mean((t - mu) ** 2, -1, keepdims=True)
            t = (t - mu) / jnp.sqrt(var + 1e-05) * ln_g + ln_b
            cls_tok = jnp.broadcast_to(cls, (t.shape[0], 1, D))
            return jnp.concatenate([cls_tok, t], axis=1)
        key = jax.random.key(seed)
        ks = jax.random.split(key, 32)

        def rn(i, shape, s=0.02):
            return jax.random.normal(ks[i], shape, jnp.float32) * s
        KW = IN * 4 ** LEVELS
        return {'x': jax.random.normal(ks[0], (B, IN, IMG, IMG), jnp.float32), 'pl_w': rn(1, (D, IN, PATCH, PATCH)), 'pl_b': rn(2, (D,)), 'pl_dw': rn(3, (D, 1, 3, 3)), 'pl_pw': rn(4, (D, D, 1, 1)), 'pl_pwb': rn(5, (D,)), 'pg_w1': rn(6, (D, KW, 1, 1)), 'pg_b1': rn(7, (D,)), 'pg_dw': rn(8, (D, 1, 3, 3)), 'pg_pw': rn(9, (D, D, 1, 1)), 'pg_pwb': rn(10, (D,)), 'pg_w2': rn(11, (D, D, 1, 1)), 'pg_b2': rn(12, (D,)), 'alpha': jnp.zeros((1, D, 1, 1), jnp.float32), 'f1_dw': rn(13, (D, 1, 3, 3)), 'f1_pw': rn(14, (D, D, 1, 1)), 'f1_pwb': rn(15, (D,)), 'f2_dw': rn(16, (D, 1, 3, 3)), 'f2_pw': rn(17, (D, D, 1, 1)), 'f2_pwb': rn(18, (D,)), 'f3_dw': rn(19, (D, 1, 3, 3)), 'f3_pw': rn(20, (D, D, 1, 1)), 'f3_pwb': rn(21, (D,)), 'ln_g': jnp.ones((D,), jnp.float32), 'ln_b': jnp.zeros((D,), jnp.float32), 'cls': rn(22, (1, 1, D))}
    _L0_tok_all = _L0_tok_setup()
    _L0_tok_in = {k: v for k, v in _L0_tok_all.items() if k in ('pl_w', 'pl_b', 'pl_dw', 'pl_pw', 'pl_pwb', 'pg_w1', 'pg_b1', 'pg_dw', 'pg_pw', 'pg_pwb', 'pg_w2', 'pg_b2', 'alpha', 'f1_dw', 'f1_pw', 'f1_pwb', 'f2_dw', 'f2_pw', 'f2_pwb', 'f3_dw', 'f3_pw', 'f3_pwb', 'ln_g', 'ln_b', 'cls')}
    del _L0_tok_all

    def _L0_attn_setup():
        import jax, jax.numpy as jnp
        import numpy as np
        B, N, C = (64, 80, 192)
        NUM_HEADS = 12
        LENS_Z = 64
        SCALE = (C // NUM_HEADS) ** (-0.5)
        key = jax.random.key(seed)
        k1, k2, k3 = jax.random.split(key, 3)
        x = jax.random.normal(k1, (B, N, C), dtype=jnp.float32)
        proj_w = jax.random.normal(k2, (C, C), dtype=jnp.float32) * 0.02
        proj_b = jax.random.normal(k3, (C,), dtype=jnp.float32) * 0.02
        return {'x': x, 'proj_w': proj_w, 'proj_b': proj_b}
    _L0_attn_all = _L0_attn_setup()
    _L0_attn_in = {k: v for k, v in _L0_attn_all.items() if k in ('proj_w', 'proj_b')}
    del _L0_attn_all

    def _L0_ffn_setup():
        import jax, jax.numpy as jnp
        import numpy as np
        B, N, D, E, F, K = (2, 512, 192, 8, 768, 2)
        V_MAX = 3.0
        FEAT_CLAMP = 10.0

        def bk_green_diag(a):
            aT = jnp.swapaxes(a, 0, 1)

            def step(c, ai):
                d = ai - 1.0 / c
                return (d, d)
            d0 = aT[0]
            _, d_rest = jax.lax.scan(step, d0, aT[1:])
            d = jnp.concatenate([d0[None], d_rest], axis=0)
            eN = aT[-1]
            _, e_rest = jax.lax.scan(step, eN, aT[:-1], reverse=True)
            e = jnp.concatenate([e_rest, eN[None]], axis=0)
            G = 1.0 / (d + e - aT)
            return jnp.swapaxes(G, 0, 1)
        key = jax.random.key(seed)
        ks = jax.random.split(key, 8)
        s = lambda k, shape, sc: jax.random.normal(k, shape, jnp.float32) * sc
        return {'x': s(ks[0], (B, N, D), 1.0), 'v_w': s(ks[1], (D,), 0.02), 'v_b': jnp.zeros((), jnp.float32), 'gate_w': s(ks[2], (D, E), 0.02), 'gate_b': jnp.zeros((E,), jnp.float32), 'w1': s(ks[3], (E, D, F), 0.02), 'b1': jnp.zeros((E, F), jnp.float32), 'w2': s(ks[4], (E, F, D), 0.02), 'b2': jnp.zeros((E, D), jnp.float32), 'out_w': s(ks[5], (2, D), 0.02), 'out_b': jnp.zeros((D,), jnp.float32), 'bk_scale': jnp.ones((D,), jnp.float32)}
    _L0_ffn_all = _L0_ffn_setup()
    _L0_ffn_in = {k: v for k, v in _L0_ffn_all.items() if k in ('v_w', 'v_b', 'gate_w', 'gate_b', 'w1', 'b1', 'w2', 'b2', 'out_w', 'out_b', 'bk_scale')}
    del _L0_ffn_all
    return {'x': x, 'L0_tok_pl_w': _L0_tok_in['pl_w'], 'L0_tok_pl_b': _L0_tok_in['pl_b'], 'L0_tok_pl_dw': _L0_tok_in['pl_dw'], 'L0_tok_pl_pw': _L0_tok_in['pl_pw'], 'L0_tok_pl_pwb': _L0_tok_in['pl_pwb'], 'L0_tok_pg_w1': _L0_tok_in['pg_w1'], 'L0_tok_pg_b1': _L0_tok_in['pg_b1'], 'L0_tok_pg_dw': _L0_tok_in['pg_dw'], 'L0_tok_pg_pw': _L0_tok_in['pg_pw'], 'L0_tok_pg_pwb': _L0_tok_in['pg_pwb'], 'L0_tok_pg_w2': _L0_tok_in['pg_w2'], 'L0_tok_pg_b2': _L0_tok_in['pg_b2'], 'L0_tok_alpha': _L0_tok_in['alpha'], 'L0_tok_f1_dw': _L0_tok_in['f1_dw'], 'L0_tok_f1_pw': _L0_tok_in['f1_pw'], 'L0_tok_f1_pwb': _L0_tok_in['f1_pwb'], 'L0_tok_f2_dw': _L0_tok_in['f2_dw'], 'L0_tok_f2_pw': _L0_tok_in['f2_pw'], 'L0_tok_f2_pwb': _L0_tok_in['f2_pwb'], 'L0_tok_f3_dw': _L0_tok_in['f3_dw'], 'L0_tok_f3_pw': _L0_tok_in['f3_pw'], 'L0_tok_f3_pwb': _L0_tok_in['f3_pwb'], 'L0_tok_ln_g': _L0_tok_in['ln_g'], 'L0_tok_ln_b': _L0_tok_in['ln_b'], 'L0_tok_cls': _L0_tok_in['cls'], 'L0_attn_proj_w': _L0_attn_in['proj_w'], 'L0_attn_proj_b': _L0_attn_in['proj_b'], 'L0_ffn_v_w': _L0_ffn_in['v_w'], 'L0_ffn_v_b': _L0_ffn_in['v_b'], 'L0_ffn_gate_w': _L0_ffn_in['gate_w'], 'L0_ffn_gate_b': _L0_ffn_in['gate_b'], 'L0_ffn_w1': _L0_ffn_in['w1'], 'L0_ffn_b1': _L0_ffn_in['b1'], 'L0_ffn_w2': _L0_ffn_in['w2'], 'L0_ffn_b2': _L0_ffn_in['b2'], 'L0_ffn_out_w': _L0_ffn_in['out_w'], 'L0_ffn_out_b': _L0_ffn_in['out_b'], 'L0_ffn_bk_scale': _L0_ffn_in['bk_scale']}

def reference(x, L0_tok_pl_w, L0_tok_pl_b, L0_tok_pl_dw, L0_tok_pl_pw, L0_tok_pl_pwb, L0_tok_pg_w1, L0_tok_pg_b1, L0_tok_pg_dw, L0_tok_pg_pw, L0_tok_pg_pwb, L0_tok_pg_w2, L0_tok_pg_b2, L0_tok_alpha, L0_tok_f1_dw, L0_tok_f1_pw, L0_tok_f1_pwb, L0_tok_f2_dw, L0_tok_f2_pw, L0_tok_f2_pwb, L0_tok_f3_dw, L0_tok_f3_pw, L0_tok_f3_pwb, L0_tok_ln_g, L0_tok_ln_b, L0_tok_cls, L0_attn_proj_w, L0_attn_proj_b, L0_ffn_v_w, L0_ffn_v_b, L0_ffn_gate_w, L0_ffn_gate_b, L0_ffn_w1, L0_ffn_b1, L0_ffn_w2, L0_ffn_b2, L0_ffn_out_w, L0_ffn_out_b, L0_ffn_bk_scale):
    import jax
    import jax.numpy as jnp

    def _L0_tok_ref(x, pl_w, pl_b, pl_dw, pl_pw, pl_pwb, pg_w1, pg_b1, pg_dw, pg_pw, pg_pwb, pg_w2, pg_b2, alpha, f1_dw, f1_pw, f1_pwb, f2_dw, f2_pw, f2_pwb, f3_dw, f3_pw, f3_pwb, ln_g, ln_b, cls):
        import jax, jax.numpy as jnp
        import numpy as np
        B, IN, IMG = (64, 3, 224)
        PATCH, LEVELS, D = (16, 4, 192)
        ISQ2 = 0.7071067811865476
        DN = ('NCHW', 'OIHW', 'NCHW')

        def conv(x, w, b=None, stride=1, pad=((0, 0), (0, 0)), groups=1):
            y = jax.lax.conv_general_dilated(x, w, (stride, stride), pad, dimension_numbers=DN, feature_group_count=groups)
            return y if b is None else y + b[None, :, None, None]

        def dwconv(x, wd, wp, bp):
            y = conv(x, wd, pad=((1, 1), (1, 1)), groups=x.shape[1])
            return conv(y, wp, bp)

        def haar_dwt2(x):
            xe, xo = (x[..., ::2], x[..., 1::2])
            lo_w, hi_w = ((xe + xo) * ISQ2, (xe - xo) * ISQ2)

            def split_h(t):
                te, to = (t[..., ::2, :], t[..., 1::2, :])
                return ((te + to) * ISQ2, (te - to) * ISQ2)
            ll, lh = split_h(lo_w)
            hl, hh = split_h(hi_w)
            return (ll, lh, hl, hh)

        def wavelet_packet(x):
            f = x
            for _ in range(LEVELS):
                b, k, h, w = f.shape
                ll, lh, hl, hh = haar_dwt2(f)
                bands = jnp.stack([ll, lh, hl, hh], axis=1)
                bands = bands.reshape(b, 4, k // IN, IN, h // 2, w // 2)
                f = jnp.transpose(bands, (0, 2, 1, 3, 4, 5)).reshape(b, 4 * k, h // 2, w // 2)
            return f

        def gelu(x):
            return jax.nn.gelu(x, approximate=False)

        def forward(x, pl_w, pl_b, pl_dw, pl_pw, pl_pwb, pg_w1, pg_b1, pg_dw, pg_pw, pg_pwb, pg_w2, pg_b2, alpha, f1_dw, f1_pw, f1_pwb, f2_dw, f2_pw, f2_pwb, f3_dw, f3_pw, f3_pwb, ln_g, ln_b, cls):
            loc = conv(x, pl_w, pl_b, stride=PATCH)
            loc = dwconv(gelu(loc), pl_dw, pl_pw, pl_pwb)
            g = wavelet_packet(x)
            g = gelu(conv(g, pg_w1, pg_b1))
            g = gelu(dwconv(g, pg_dw, pg_pw, pg_pwb))
            glob = conv(g, pg_w2, pg_b2)
            gate = 0.5 * (jnp.tanh(alpha) + 1.0)
            h = (1.0 - gate) * loc + gate * glob
            h = jax.nn.relu(dwconv(h, f1_dw, f1_pw, f1_pwb))
            h = jax.nn.relu(dwconv(h, f2_dw, f2_pw, f2_pwb))
            h = dwconv(loc + h, f3_dw, f3_pw, f3_pwb)
            t = jnp.transpose(h.reshape(h.shape[0], D, -1), (0, 2, 1))
            mu = jnp.mean(t, -1, keepdims=True)
            var = jnp.mean((t - mu) ** 2, -1, keepdims=True)
            t = (t - mu) / jnp.sqrt(var + 1e-05) * ln_g + ln_b
            cls_tok = jnp.broadcast_to(cls, (t.shape[0], 1, D))
            return jnp.concatenate([cls_tok, t], axis=1)
        return forward(x, pl_w, pl_b, pl_dw, pl_pw, pl_pwb, pg_w1, pg_b1, pg_dw, pg_pw, pg_pwb, pg_w2, pg_b2, alpha, f1_dw, f1_pw, f1_pwb, f2_dw, f2_pw, f2_pwb, f3_dw, f3_pw, f3_pwb, ln_g, ln_b, cls)

    def _L0_attn_ref(x, proj_w, proj_b):
        import jax, jax.numpy as jnp
        import numpy as np
        B, N, C = (64, 80, 192)
        NUM_HEADS = 12
        LENS_Z = 64
        SCALE = (C // NUM_HEADS) ** (-0.5)
        q = x[:, :LENS_Z]
        k = x[:, LENS_Z:]
        v = k
        attn = jnp.einsum('bqc,bkc->bqk', q, k) * SCALE
        attn = jax.nn.softmax(attn, axis=-1)
        out = jnp.einsum('bqk,bkc->bqc', attn, v)
        out = jnp.transpose(out, (0, 2, 1)).reshape(out.shape[0], -1, C)
        out = out @ proj_w.T + proj_b
        return jnp.concatenate([out, k], axis=1)

    def _L0_ffn_ref(x, v_w, v_b, gate_w, gate_b, w1, b1, w2, b2, out_w, out_b, bk_scale):
        import jax, jax.numpy as jnp
        import numpy as np
        B, N, D, E, F, K = (2, 512, 192, 8, 768, 2)
        V_MAX = 3.0
        FEAT_CLAMP = 10.0

        def bk_green_diag(a):
            aT = jnp.swapaxes(a, 0, 1)

            def step(c, ai):
                d = ai - 1.0 / c
                return (d, d)
            d0 = aT[0]
            _, d_rest = jax.lax.scan(step, d0, aT[1:])
            d = jnp.concatenate([d0[None], d_rest], axis=0)
            eN = aT[-1]
            _, e_rest = jax.lax.scan(step, eN, aT[:-1], reverse=True)
            e = jnp.concatenate([e_rest, eN[None]], axis=0)
            G = 1.0 / (d + e - aT)
            return jnp.swapaxes(G, 0, 1)
        v = jnp.clip(x @ v_w + v_b, -V_MAX, V_MAX)
        a = (-2.0 + v).astype(jnp.complex64) - 1j
        G = bk_green_diag(a)
        feats = jnp.stack([G.real, G.imag], axis=-1)
        logits = x @ gate_w + gate_b
        probs = jax.nn.softmax(logits, axis=-1)
        topv, topi = jax.lax.top_k(probs, K)
        topv = topv / jnp.sum(topv, axis=-1, keepdims=True)
        comb = jnp.sum(topv[..., None] * jax.nn.one_hot(topi, E, dtype=x.dtype), axis=2)
        h = jax.nn.gelu(jnp.einsum('bnd,edf->bnef', x, w1) + b1)
        y = jnp.einsum('bnef,efd->bned', h, w2) + b2
        ffn_out = jnp.einsum('bne,bned->bnd', comb, y)
        feats_c = jnp.clip(feats, -FEAT_CLAMP, FEAT_CLAMP)
        spec_out = feats_c @ out_w + out_b
        return ffn_out + bk_scale * spec_out
    h = _L0_tok_ref(x, L0_tok_pl_w, L0_tok_pl_b, L0_tok_pl_dw, L0_tok_pl_pw, L0_tok_pl_pwb, L0_tok_pg_w1, L0_tok_pg_b1, L0_tok_pg_dw, L0_tok_pg_pw, L0_tok_pg_pwb, L0_tok_pg_w2, L0_tok_pg_b2, L0_tok_alpha, L0_tok_f1_dw, L0_tok_f1_pw, L0_tok_f1_pwb, L0_tok_f2_dw, L0_tok_f2_pw, L0_tok_f2_pwb, L0_tok_f3_dw, L0_tok_f3_pw, L0_tok_f3_pwb, L0_tok_ln_g, L0_tok_ln_b, L0_tok_cls)
    h = _layernorm(h + _L0_attn_ref(h, L0_attn_proj_w, L0_attn_proj_b), axis=-1)
    h = _layernorm(h + _L0_ffn_ref(h, L0_ffn_v_w, L0_ffn_v_b, L0_ffn_gate_w, L0_ffn_gate_b, L0_ffn_w1, L0_ffn_b1, L0_ffn_w2, L0_ffn_b2, L0_ffn_out_w, L0_ffn_out_b, L0_ffn_bk_scale), axis=-1)
    return h

_drawn_inputs = setup_inputs


def setup_inputs(seed=0):
    import zlib

    import numpy as np

    out = dict(_drawn_inputs(seed))
    spreads = {'L0_tok_alpha': (0.0, 0.8),
     'L0_tok_ln_g': (1.0, 0.2),
     'L0_tok_ln_b': (0.0, 0.1),
     'L0_ffn_gate_b': (0.0, 0.1),
     'L0_ffn_b1': (0.0, 0.344),
     'L0_ffn_b2': (0.0, 0.1),
     'L0_ffn_out_b': (0.0, 0.1),
     'L0_ffn_bk_scale': (1.0, 0.6)}
    factors = {'x': 8.0,
     'L0_tok_pl_w': 8.0,
     'L0_tok_pl_b': 55.089,
     'L0_tok_pl_dw': 8.0,
     'L0_tok_pl_pw': 8.0,
     'L0_tok_pl_pwb': 31.672,
     'L0_tok_pg_w1': 8.0,
     'L0_tok_pg_b1': 185.807,
     'L0_tok_pg_dw': 8.0,
     'L0_tok_pg_pw': 8.0,
     'L0_tok_pg_pwb': 64.0,
     'L0_tok_pg_w2': 8.0,
     'L0_tok_pg_b2': 177.604,
     'L0_tok_f1_dw': 8.0,
     'L0_tok_f1_pw': 8.0,
     'L0_tok_f1_pwb': 64.0,
     'L0_tok_f2_dw': 8.0,
     'L0_tok_f2_pw': 8.0,
     'L0_tok_f2_pwb': 48.211,
     'L0_tok_f3_dw': 2.721,
     'L0_tok_f3_pw': 3.219,
     'L0_ffn_v_w': 8.0,
     'L0_ffn_out_w': 5.012,
     'L0_tok_f3_pwb': 4.836}
    for name, (base, spread) in spreads.items():
        noise = np.random.default_rng([zlib.crc32(name.encode()), seed]).standard_normal(out[name].shape)
        drawn = base * np.exp(spread * noise) if base else spread * noise
        out[name] = jnp.asarray(drawn.astype(out[name].dtype))
    for name, factor in factors.items():
        out[name] = (out[name] * factor).astype(out[name].dtype)
    return out
```

```python
from contextlib import ExitStack

import numpy as np

import concourse.bass as bass
from concourse import mybir

F32 = mybir.dt.float32
F32R = mybir.dt.float32r
ALU = mybir.AluOpType
ACT = mybir.ActivationFunctionType
AX = mybir.AxisListType

P = 128
B, CIN, PATCH, G = 16, 3, 16, 6
NPX = G * G * B
HPX = NPX // 2
D = 192
DB = D - P
KP = CIN * PATCH * PATCH
KT = KP // P
TOK = NPX + B
HT = TOK // 2
NT = -(-TOK // P)
LAST = NPX - (NT - 1) * P
SEQ = G * G + 1
E, F = 8, 768
FK = F // P
EPS = 1e-5
LAG = 2
RING = 3
TAPS = [(0, 0)] + [(dy, dx) for dy in (-1, 0, 1) for dx in (-1, 0, 1) if (dy, dx) != (0, 0)]

V = {}
_n = 0
for _name, _w in [("dw1", 27), ("dwf", 54), ("bias1", 3), ("bias2", 3), ("b_w2", 2), ("alpha", 2), ("fb", 6),
                  ("v_w", 2), ("bk", 2), ("out_b", 2), ("gate_w", 16), ("v_b", 1), ("b1", E * FK)]:
    V[_name] = _n
    _n += _w
NVEC = _n


def tower(nc, x, vec, rows, had, w1t, plw, pw, projw, cls, ident, pair, sel, w1, w2, b2, outw, out):
    with ExitStack() as ctx:
        def sb(name, shape, dt=F32):
            return ctx.enter_context(nc.sbuf_tensor(name, shape, dt))

        def sem(name):
            return ctx.enter_context(nc.semaphore(name))

        ps = ctx.enter_context(nc.psum_tensor("ps", [P, 8, 512], F32))
        psf = ps[:].rearrange("p k n -> p (k n)")

        vecs = sb("vecs", [P, NVEC])
        rowb = sb("rowb", [P, 2 * D + E])
        had_s = sb("had_s", [P, 2, 256])
        w1t_s = sb("w1t_s", [P, 2, CIN * D])
        x_s = sb("x_s", [P, KT, NPX])
        embed = sb("embed", [P, KT, 2 * D])
        pw_s = sb("pw_s", [P, 6, 2, D])
        proj_s = sb("proj_s", [P, 2, D])
        projb_s = sb("projb_s", [1, D])
        id_s = sb("id_s", [P, P])
        pair_s = sb("pair_s", [P, DB])
        sel_s = sb("sel_s", [2 * E, E * P])
        cls_s = sb("cls_s", [P, D])
        conv = sb("conv", [P, 3, 3, NPX])
        act_a, act_b = conv[:, 0], conv[:, 1]
        loc = conv[:, 2]
        glob = sb("glob", [P, 2, NPX])
        gate = sb("gate", [P, 8])
        zt = sb("zt", [P, NT, D])
        ht = sb("ht", [P, NT, 256])
        stats = sb("stats", [P, NT, 6])
        mv = sb("mv", [P, NT, 2])
        var = sb("var", [P, NT])
        rstd = sb("rstd", [P, NT])
        neghalf = sb("neghalf", [P, NT])
        zero = sb("zero", [P, P])
        ones = sb("ones", [1, P])
        attn = sb("attn", [P, D])
        xf = sb("xf", [P, 2, NT * P])
        xh = sb("xh", [P, TOK], F32R)
        xl = sb("xl", [P, TOK], F32R)
        xb = sb("xb", [P, TOK], F32R)
        xbh = sb("xbh", [P, TOK], F32R)
        lg = sb("lg", [P, NT, E])
        lgt = sb("lgt", [P, NT, E, E])
        lge = sb("lge", [P, NT, E, E])
        rk = sb("rk", [P, NT, E])
        sc = sb("sc", [P, 4, NT])
        comb = sb("comb", [P, NT, E])
        comb2 = sb("comb2", [P, NT, 2 * E], F32R)
        comb2f = sb("comb2f", [P, NT, 2 * E])
        combt = sb("combt", [2 * E, NT * P], F32R)
        combtf = sb("combtf", [2 * E, NT * P])
        selr = sb("selr", [2 * E, E * P], F32R)
        cb = conv[:].rearrange("p a t c -> p (a t c)")[:, 0:E * TOK].rearrange("p (e c) -> p e c", e=E)
        vw64 = sb("vw64", [P, 2, 64])
        w1raw = sb("w1raw", [P, 2, 2, F])
        w2raw = sb("w2raw", [P, 2, FK, D])
        w1h = sb("w1h", [P, 2, 2, F], F32R)
        w1l = sb("w1l", [P, 2, 2, F], F32R)
        w2s = sb("w2s", [P, 2, FK, 2 * D], F32R)
        hg = sb("hg", [P, 2, TOK])
        hw = sb("hw", [P, 2, TOK])
        hh = sb("hh", [P, RING, TOK], F32R)
        hl = sb("hl", [P, RING, TOK], F32R)
        b2_s = sb("b2_s", [2 * E, 2 * P])
        yt = x_s[:].rearrange("p k c -> p (k c)")[:, 0:2 * TOK].rearrange("p (t c) -> p t c", t=2)
        vm = sb("vm", [64, TOK])
        vseq = sb("vseq", [64, SEQ])
        ar = sb("ar", [64, SEQ, 2])
        tr = sb("tr", [64, SEQ + 2, 2])
        sw = sb("sw", [64, 2, 2])
        phi = sb("phi", [B, SEQ, 2])
        zz = sb("zz", [B, 6, SEQ])
        wi = sb("wi", [B, 8])
        ft = sb("ft", [B, 2, SEQ])
        gm = sb("gm", [48, TOK])
        ow = sb("ow", [48, 2 * P])
        bkr = sb("bkr", [48, D])

        d_had, d_vec, d_plw, d_pw, d_misc, d_proj, d_ffn, d_cls, d_rows = [
            sem("ld_" + n) for n in ("had", "vec", "plw", "pw", "misc", "proj", "ffn", "cls", "rows")]
        d_x = [sem(f"ld_x{k}") for k in range(KT)]
        d_w = [sem("ld_w0"), sem("ld_w1")]
        d_out = sem("stored")
        had_mm = sem("had_mm")
        had_cp = sem("had_cp")
        emb_mm = sem("emb_mm")
        gelu1 = sem("gelu1")
        dw_done = sem("dw_done")
        pw_mm = sem("pw_mm")
        pw_ev = sem("pw_ev")
        gates = sem("gates")
        mixed = sem("mixed")
        v_done = sem("v_done")
        a_done = sem("a_done")
        p_done = sem("p_done")
        zeroed = sem("zeroed")
        attn_mm = sem("attn_mm")
        tok_mm = sem("tok_mm")
        var_rdy = sem("var_rdy")
        rstd_rdy = sem("rstd_rdy")
        ht_rdy = sem("ht_rdy")
        xt_mm = sem("xt_mm")
        xf_rdy = sem("xf_rdy")
        xs_rdy = sem("xs_rdy")
        lg_mm = sem("lg_mm")
        lg_max = sem("lg_max")
        lg_exp = sem("lg_exp")
        comb_rdy = sem("comb_rdy")
        combt_mm = sem("combt_mm")
        combt_rdy = sem("combt_rdy")
        v_mm = sem("v_mm")
        v_ev = sem("v_ev")
        vseq_rdy = sem("vseq_rdy")
        cb_mm = sem("cb_mm")
        cb_even = sem("cb_even")
        cb_odd = sem("cb_odd")
        hi_rdy = sem("hi_rdy")
        lo_rdy = sem("lo_rdy")
        l1_mm = sem("l1_mm")
        h_read = sem("h_read")
        hw_rdy = sem("hw_rdy")
        hh_rdy = sem("hh_rdy")
        hl_rdy = sem("hl_rdy")
        l2_mm = sem("l2_mm")
        bk_w = sem("bk_w")
        bk_inv = sem("bk_inv")
        bk_rdy = sem("bk_rdy")
        ow_zero = sem("ow_zero")
        ow_rdy = sem("ow_rdy")
        y_mm = sem("y_mm")
        y_ev = sem("y_ev")
        yt_mm = sem("yt_mm")
        fin_rdy = sem("fin_rdy")

        def vcol(name, i=0, rows=slice(0, P)):
            return vecs[rows, V[name] + i:V[name] + i + 1]

        A, LO, HI = slice(0, P), slice(0, DB), slice(DB, P)

        block = ctx.enter_context(nc.Block())

        def load_expert(q, e, slot):
            q.dma_start(w1raw[:, slot, 0, :], w1[e, 0:P, :]).then_inc(d_w[slot], 16)
            q.dma_start(w1raw[LO, slot, 1, :], w1[e, P:D, :]).then_inc(d_w[slot], 16)
            q.dma_start(w1raw[HI, slot, 1, :], w1[e, P:D, :]).then_inc(d_w[slot], 16)
            q.dma_start(w2raw[:, slot, :, :], w2[e]).then_inc(d_w[slot], 16)

        @block.sync
        def _(sp):
            sp.dma_start(had_s[:], had).then_inc(d_had, 16)
            for k in range(KT):
                sp.dma_start(x_s[:, k, :], x[k]).then_inc(d_x[k], 16)
            sp.dma_start(pw_s[:], pw).then_inc(d_pw, 16)
            sp.dma_start(id_s[:], ident).then_inc(d_misc, 16)
            sp.dma_start(pair_s[:], pair).then_inc(d_misc, 16)
            sp.dma_start(sel_s[:], sel).then_inc(d_misc, 16)
            load_expert(sp, 0, 0)
            load_expert(sp, 1, 1)
            for e in range(2, E):
                sp.wait_ge(hi_rdy, 2 * (e - 1))
                sp.wait_ge(lo_rdy, 3 * (e - 1))
                load_expert(sp, e, e % 2)
            for t in range(NT):
                sp.wait_ge(fin_rdy, t + 1)
                n = P if t < NT - 1 else TOK - P * (NT - 1)
                sp.dma_start(out[t * P:t * P + n, :], zt[0:n, t, :]).then_inc(d_out, 16)
            sp.wait_ge(d_out, 16 * NT)

        def spectral(pool):
            n = 4
            pool.wait_ge(vseq_rdy, 2)
            pool.wait_ge(p_done, n)
            for i in range(SEQ):
                nc.gpsimd.tensor_tensor(sw[:, 0, :], tr[:, i, :], tr[:, i + 1, :], ALU.add).then_inc(p_done, 1)
                nc.gpsimd.tensor_tensor(sw[:, 1, :], ar[:, i, :], tr[:, i + 1, ::-1], ALU.mult).then_inc(p_done, 1)
                n += 2
                pool.wait_ge(p_done, n)
                nc.gpsimd.tensor_tensor(tr[:, i + 2, :], sw[:, 0, :], sw[:, 1, :], ALU.add).then_inc(p_done, 1)
                n += 1
                pool.wait_ge(p_done, n)

            def link(ins):
                nonlocal n
                ins.then_inc(p_done, 1)
                n += 1
                pool.wait_ge(p_done, n)

            link(nc.gpsimd.tensor_scalar(wi[:, 0:2], tr[0:B, SEQ + 1, :], 2.0 ** -60, None, ALU.mult))
            link(nc.gpsimd.tensor_tensor(wi[:, 2:4], wi[:, 0:2], wi[:, 0:2], ALU.mult))
            nc.gpsimd.tensor_tensor(wi[:, 4:5], wi[:, 2:3], wi[:, 3:4], ALU.add).then_inc(bk_w, 1)
            link(nc.gpsimd.tensor_copy(phi[:], tr[32:32 + B, SEQ:0:-1, :]))
            th = tr[0:B, 1:SEQ + 1, :]
            link(nc.gpsimd.tensor_tensor(zz[:, 0, :], th[:, :, 0], phi[:, :, 0], ALU.mult))
            link(nc.gpsimd.tensor_tensor(zz[:, 1, :], th[:, :, 1], phi[:, :, 1], ALU.mult))
            link(nc.gpsimd.tensor_tensor(zz[:, 2, :], th[:, :, 0], phi[:, :, 1], ALU.mult))
            link(nc.gpsimd.tensor_tensor(zz[:, 3, :], th[:, :, 1], phi[:, :, 0], ALU.mult))
            link(nc.gpsimd.tensor_tensor(zz[:, 0, :], zz[:, 0, :], zz[:, 1, :], ALU.subtract))
            link(nc.gpsimd.tensor_tensor(zz[:, 1, :], zz[:, 2, :], zz[:, 3, :], ALU.add))
            pool.wait_ge(bk_inv, 1)
            link(nc.gpsimd.tensor_scalar(wi[:, 6:8], wi[:, 0:2], wi[:, 5:6], 2.0 ** -60, ALU.mult, ALU.mult))
            link(nc.gpsimd.tensor_scalar(zz[:, 2, :], zz[:, 0, :], wi[:, 6:7], None, ALU.mult))
            link(nc.gpsimd.tensor_scalar(zz[:, 3, :], zz[:, 1, :], wi[:, 7:8], None, ALU.mult))
            link(nc.gpsimd.tensor_scalar(zz[:, 4, :], zz[:, 1, :], wi[:, 6:7], None, ALU.mult))
            link(nc.gpsimd.tensor_scalar(zz[:, 5, :], zz[:, 0, :], wi[:, 7:8], None, ALU.mult))
            link(nc.gpsimd.tensor_tensor(ft[:, 0, :], zz[:, 5, :], zz[:, 4, :], ALU.subtract))
            link(nc.gpsimd.tensor_tensor(ft[:, 1, :], zz[:, 2, :], zz[:, 3, :], ALU.add))
            link(nc.gpsimd.tensor_scalar(ft[:], ft[:], 10.0, -10.0, ALU.min, ALU.max))
            for f in range(2):
                r = slice(32 * f, 32 * f + B)
                mask = id_s[0:B, 0:B]
                nc.gpsimd.tensor_tensor(gm[r, 0:NPX].rearrange("p (n b) -> p n b", b=B),
                                        ft[:, f, 1:SEQ].unsqueeze(2).to_broadcast([B, SEQ - 1, B]),
                                        mask.unsqueeze(1).to_broadcast([B, SEQ - 1, B]),
                                        ALU.mult).then_inc(bk_rdy, 1)
                nc.gpsimd.tensor_tensor(gm[r, NPX:TOK], ft[:, f, 0:1].to_broadcast([B, B]), mask,
                                        ALU.mult).then_inc(bk_rdy, 1)

        @block.gpsimd
        def _(pool):
            nc.gpsimd.memset(neghalf[:], -0.5).then_inc(p_done, 1)
            nc.gpsimd.memset(tr[:], 0.0).then_inc(p_done, 1)
            nc.gpsimd.memset(gm[:], 0.0).then_inc(p_done, 1)
            nc.gpsimd.memset(ow[:], 0.0).then_inc(ow_zero, 1)
            pool.wait_ge(p_done, 3)
            nc.gpsimd.memset(tr[:, 1:2, 0:1], 1.0).then_inc(p_done, 1)
            for n in range(3):
                pool.wait_ge(var_rdy, n + 1)
                nc.gpsimd.tensor_tensor(rstd[:], var[:], neghalf[:], ALU.pow).then_inc(rstd_rdy, 1)
                if n == 1:
                    spectral(pool)

        @block.scalar
        def _(act):
            act.dma_start(w1t_s[:], w1t).then_inc(d_had, 16)
            act.dma_start(vecs[:], vec).then_inc(d_vec, 16)
            for k in range(KT):
                act.dma_start(embed[:, k, 0:D], plw[k]).then_inc(d_plw, 16)
            act.dma_start(proj_s[:], projw[:, 0:2 * D].rearrange("p (t d) -> p t d", t=2)).then_inc(d_proj, 16)
            act.dma_start(projb_s[:], projw[0:1, 2 * D:3 * D]).then_inc(d_proj, 16)
            act.dma_start(cls_s[LAST:LAST + B, :], cls.to_broadcast([B, D])).then_inc(d_cls, 16)
            act.dma_start(rowb[:], rows[0:1, 0:2 * D + E].to_broadcast([P, 2 * D + E])).then_inc(d_rows, 16)
            act.wait_ge(ow_zero, 1)
            for f in range(2):
                act.dma_start(ow[32 * f:32 * f + B, 0:D], outw[f:f + 1, :].to_broadcast([B, D])).then_inc(d_ffn, 16)
                act.dma_start(bkr[32 * f:32 * f + B, :],
                              rows[0:1, 2 * D + E:3 * D + E].to_broadcast([B, D])).then_inc(d_ffn, 16)
                act.dma_start(b2_s[E * f:E * f + E, 0:D], b2).then_inc(d_ffn, 16)
            act.wait_ge(d_vec, 16)
            nc.scalar.activation(gate[:, 0:2], vecs[:, V["alpha"]:V["alpha"] + 2], ACT.Tanh).then_inc(a_done, 1)
            for pt in range(2):
                act.wait_ge(had_mm, pt + 1)
                b = 6 if pt == 0 else 4
                nc.scalar.copy(embed[:, pt:pt + 3:2, D:2 * D],
                               ps[:, b, 0:2 * D].rearrange("p (c n) -> p c n", c=2)).then_inc(had_cp, 1)
                nc.scalar.copy(embed[:, 4 + pt, D:2 * D], ps[:, b + 1, 0:D]).then_inc(had_cp, 1)
            act.wait_ge(emb_mm, 1)
            for t in (1, 0, 2):
                nc.scalar.activation(act_a[:, t, :].rearrange("p (h n) -> p h n", h=2), ps[:, 2 * t:2 * t + 2, 0:HPX],
                                     ACT.Gelu, bias=vcol("bias1", t)).then_inc(gelu1, 1)

            def evacuate(bank, dst, rows_, func, bias, scale=1.0):
                nc.scalar.activation(dst.rearrange("p (h n) -> p h n", h=2), ps[rows_, bank:bank + 2, 0:HPX], func,
                                     bias=bias, scale=scale).then_inc(pw_ev, 1)

            act.wait_ge(pw_mm, 1)
            evacuate(2, loc[:, 2, :], A, ACT.Gelu, vcol("bias2", 2))
            evacuate(0, loc[HI, 1, :], HI, ACT.Gelu, vcol("bias2", 1, HI))
            act.wait_ge(pw_mm, 2)
            evacuate(6, loc[:, 0, :], A, ACT.Identity, vcol("bias2", 0))
            evacuate(0, loc[LO, 1, :], LO, ACT.Identity, vcol("bias2", 1, LO))
            act.wait_ge(gates, 1)
            act.wait_ge(pw_mm, 3)
            evacuate(4, glob[:, 0, :], A, ACT.Identity, gate[:, 6:7], gate[:, 2:3])
            evacuate(6, glob[LO, 1, :], LO, ACT.Identity, gate[LO, 7:8], gate[LO, 3:4])
            for f in range(3):
                b = 4 if f == 1 else 0
                act.wait_ge(pw_mm, 4 + f)
                fn = ACT.Relu if f < 2 else ACT.Identity
                evacuate(b, act_b[:, 0, :], A, fn, vcol("fb", 2 * f))
                evacuate(b + 2, act_b[LO, 1, :], LO, fn, vcol("fb", 2 * f + 1, LO))
            act.wait_ge(attn_mm, 1)
            nc.scalar.copy(attn[:], ps[:, 5, 0:D]).then_inc(a_done, 1)

            def split_hi(slot, part):
                if part == 0:
                    nc.scalar.copy(w1h[:, slot, :, :], w1raw[:, slot, :, :]).then_inc(hi_rdy, 1)
                else:
                    nc.scalar.copy(w2s[:, slot, :, 0:D], w2raw[:, slot, :, :]).then_inc(hi_rdy, 1)

            act.wait_ge(d_w[0], 64)
            split_hi(0, 0)
            split_hi(0, 1)
            act.wait_ge(xt_mm, 1)
            nc.scalar.copy(xf[:, 0, :], psf[:, 6 * 512:6 * 512 + NT * P]).then_inc(xf_rdy, 1)
            act.wait_ge(xt_mm, 2)
            nc.scalar.copy(xf[LO, 1, :], psf[LO, 0:NT * P]).then_inc(xf_rdy, 1)
            nc.scalar.sem_inc(h_read, 2)
            act.wait_ge(lg_max, 1)
            nc.scalar.activation(comb[:], lg[:], ACT.Exp).then_inc(lg_exp, 1)

            def hidden(i, j, k):
                s = i * 2 * FK + (j * FK + k)
                sl = (j * FK + k)
                act.wait_ge(l1_mm, s + 1)
                nc.scalar.activation(hg[:, sl % 2, :].rearrange("p (h n) -> p h n", h=2),
                                     ps[:, 2 * (sl % 2):2 * (sl % 2) + 2, 0:HT], ACT.Gelu_apprx_tanh,
                                     bias=vecs[:, bass.ds(i * 2 * FK + (V["b1"] + j * FK + k), 1)]
                                     ).then_inc(h_read, 1)
                act.wait_ge(hw_rdy, s + 1)
                act.wait_ge(l2_mm, s + 1)
                nc.scalar.copy(hh[:, sl % RING, :], hw[:, sl % 2, :]).then_inc(hh_rdy, 1)

            def pair_of_experts(i, last):
                for j in range(2):
                    for k in range(FK):
                        hidden(i, j, k)
                        nxt = not (last and j == 1)
                        if nxt and k in (1, 3):
                            if k == 1:
                                n_ld = (i + 1) * 64 if j == 0 else (i + 2) * 64
                                act.wait_ge(d_w[1 - j], n_ld)
                                act.wait_ge(l2_mm, i * 2 * FK + (j * FK + RING))
                            split_hi(1 - j, k // 2)

            for e in range(0, E, 2):
                act.wait_ge(cb_mm, e + 1)
                nc.scalar.copy(cb[:, e, :].rearrange("p (h n) -> p h n", h=2), ps[:, 4:6, 0:HT]).then_inc(cb_even, 1)
            with act.Fori(0, E // 2 - 1) as i:
                pair_of_experts(i, False)
            pair_of_experts(E // 2 - 1, True)
            act.wait_ge(y_mm, 1)
            for t in range(2):
                nc.scalar.activation(yt[:, t, :].rearrange("p (h n) -> p h n", h=2),
                                     ps[:, 4 + 2 * t:6 + 2 * t, 0:HT], ACT.Identity,
                                     bias=gate[:, 4 + t:5 + t]).then_inc(y_ev, 1)

        @block.vector
        def _(dve):
            n = 0

            def own(ins):
                nonlocal n
                n += 1
                ins.then_inc(v_done, 1)
                return n

            def link(ins):
                dve.wait_ge(v_done, own(ins))

            nc.vector.memset(zero[:], 0.0).then_inc(zeroed, 1)
            nc.vector.memset(ones[:], 1.0).then_inc(zeroed, 1)
            nc.vector.memset(b2_s[:, D:], 0.0).then_inc(zeroed, 1)
            link(nc.vector.memset(zt[HI, NT - 1, :], 0.0))
            link(nc.vector.memset(mv[:], 0.0))
            dve.wait_ge(d_vec, 16)
            link(nc.vector.tensor_copy(vw64[:], vecs[:, V["v_w"]:V["v_w"] + 2].unsqueeze(2).to_broadcast([P, 2, 64])))
            link(nc.vector.tensor_tensor(gate[:, 4:6], vecs[:, V["bk"]:V["bk"] + 2], vecs[:, V["out_b"]:V["out_b"] + 2],
                                         ALU.mult))
            dve.wait_ge(a_done, 1)
            link(nc.vector.tensor_scalar(gate[:, 2:4], gate[:, 0:2], 1.0, 0.5, ALU.add, ALU.mult))
            link(nc.vector.tensor_scalar(gate[:, 0:2], gate[:, 2:4], -1.0, 1.0, ALU.mult, ALU.add))
            nc.vector.tensor_tensor(gate[:, 6:8], gate[:, 2:4], vecs[:, V["b_w2"]:V["b_w2"] + 2],
                                    ALU.mult).then_inc(gates, 1)

            def depthwise(src, dst, taps, tiles):
                mark = {}
                for m, (dy, dx) in enumerate(TAPS):
                    tap = (dy + 1) * 3 + dx + 1
                    y0, y1, x0, x1 = max(0, -dy), G - max(0, dy), max(0, -dx), G - max(0, dx)
                    for t, rows_ in tiles:
                        s3 = src[rows_, t, :].rearrange("p (y x) -> p y x", y=G)
                        d3 = dst[rows_, t, :].rearrange("p (y x) -> p y x", y=G)
                        o = d3[:, y0:y1, x0 * B:x1 * B]
                        a = s3[:, y0 + dy:y1 + dy, (x0 + dx) * B:(x1 + dx) * B]
                        w = vecs[rows_, taps + 9 * t + tap:taps + 9 * t + tap + 1]
                        if m == 0:
                            ins = nc.vector.tensor_scalar(o, a, w, None, ALU.mult)
                        else:
                            dve.wait_ge(v_done, mark[t])
                            ins = nc.vector.scalar_tensor_tensor(out=o, in0=a, scalar=w, in1=o, op0=ALU.mult,
                                                                 op1=ALU.add)
                        if m == len(TAPS) - 1:
                            ins.then_inc(dw_done, 1)
                        else:
                            mark[t] = own(ins)

            dve.wait_ge(gelu1, 3)
            depthwise(act_a, act_b, V["dw1"], [(2, A), (1, A), (0, A)])
            dve.wait_ge(pw_ev, 6)
            for t, rows_ in ((0, A), (1, LO)):
                own(nc.vector.scalar_tensor_tensor(out=act_a[rows_, t, :], in0=loc[rows_, t, :],
                                                   scalar=gate[rows_, t:t + 1], in1=glob[rows_, t, :],
                                                   op0=ALU.mult, op1=ALU.add))
            dve.wait_ge(v_done, n)
            two = [(0, A), (1, LO)]
            depthwise(act_a, act_b, V["dwf"], two)
            dve.wait_ge(pw_ev, 8)
            depthwise(act_b, act_a, V["dwf"] + 18, two)
            dve.wait_ge(pw_ev, 10)
            for t, rows_ in two:
                own(nc.vector.tensor_tensor(glob[rows_, t, :], act_b[rows_, t, :], loc[rows_, t, :], ALU.add))
            dve.wait_ge(v_done, n)
            depthwise(glob, act_a, V["dwf"] + 36, two)

            def norm_stats(src, tiles):
                for t, rows_ in tiles:
                    own(nc.vector.bn_stats(stats[rows_, t, :], src(t, rows_)))
                dve.wait_ge(v_done, n)
                for t, rows_ in tiles:
                    own(nc.vector.bn_aggr(mv[rows_, t, :], stats[rows_, t, :]))
                dve.wait_ge(v_done, n)
                nc.vector.tensor_scalar(var[:], mv[:, :, 1], EPS, None, ALU.add).then_inc(var_rdy, 1)

            full = [(t, A) for t in range(NT)]
            px_tiles = full[:-1] + [(NT - 1, slice(0, LAST))]
            dve.wait_ge(tok_mm, 1)
            norm_stats(lambda t, r: ps[r, t, 0:D], px_tiles)
            dve.wait_ge(rstd_rdy, 1)
            for t, r in px_tiles:
                own(nc.vector.tensor_scalar(zt[r, t, :], ps[r, t, 0:D], mv[r, t, 0:1], rstd[r, t:t + 1],
                                            ALU.subtract, ALU.mult))
            dve.wait_ge(v_done, n)
            dve.wait_ge(d_rows, 16)
            dve.wait_ge(a_done, 2)
            dve.wait_ge(d_cls, 16)
            own(nc.vector.tensor_tensor(rowb[:, D:2 * D], rowb[:, D:2 * D], attn[:], ALU.add))
            cr = slice(LAST, LAST + B)
            own(nc.vector.tensor_tensor(zt[cr, NT - 1, :], cls_s[cr, :], attn[cr, :], ALU.add))
            q = NT - 1
            own(nc.vector.tensor_tensor(zt[:, 0:q, :], zt[:, 0:q, :],
                                        rowb[:, 0:D].unsqueeze(1).to_broadcast([P, q, D]), ALU.mult))
            own(nc.vector.tensor_tensor(zt[LO, q, :], zt[LO, q, :], rowb[LO, 0:D], ALU.mult))
            dve.wait_ge(v_done, n)
            own(nc.vector.tensor_tensor(zt[:, 0:q, :], zt[:, 0:q, :],
                                        rowb[:, D:2 * D].unsqueeze(1).to_broadcast([P, q, D]), ALU.add))
            own(nc.vector.tensor_tensor(zt[LO, q, :], zt[LO, q, :], rowb[LO, D:2 * D], ALU.add))
            dve.wait_ge(v_done, n)
            norm_stats(lambda t, r: zt[r, t, :], full)
            dve.wait_ge(rstd_rdy, 2)
            for t, r in full:
                nc.vector.tensor_scalar(ht[r, t, 0:D], zt[r, t, :], mv[r, t, 0:1], rstd[r, t:t + 1],
                                        ALU.subtract, ALU.mult).then_inc(ht_rdy, 1)
                nc.vector.tensor_scalar(ht[r, t, D:256], zt[r, t, P:D], mv[r, t, 0:1], rstd[r, t:t + 1],
                                        ALU.subtract, ALU.mult).then_inc(ht_rdy, 1)
            dve.wait_ge(xf_rdy, 2)
            bank6, bank0 = psf[:, 6 * 512:6 * 512 + TOK], psf[:, 0:TOK]
            link(nc.vector.tensor_copy(xh[:], bank6))
            nc.vector.tensor_tensor(xl[:], bank6, xh[:].bitcast(F32), ALU.subtract).then_inc(xs_rdy, 1)
            link(nc.vector.tensor_copy(xbh[:], bank0))
            own(nc.vector.tensor_copy(xb[LO, :], xbh[LO, :].bitcast(F32)))
            nc.vector.tensor_tensor(xb[HI, :], psf[HI, 0:TOK], xbh[HI, :].bitcast(F32),
                                    ALU.subtract).then_inc(xs_rdy, 1)

            def split_lo(slot, part):
                if part == 0:
                    nc.vector.tensor_tensor(w1l[:, slot, :, :], w1raw[:, slot, :, :],
                                            w1h[:, slot, :, :].bitcast(F32), ALU.subtract).then_inc(lo_rdy, 1)
                else:
                    a, o = (slice(P, D), slice(D, 256)) if part == 1 else (slice(0, P), slice(256, 2 * D))
                    nc.vector.tensor_tensor(w2s[:, slot, :, o], w2raw[:, slot, :, a],
                                            w2s[:, slot, :, a].bitcast(F32), ALU.subtract).then_inc(lo_rdy, 1)

            dve.wait_ge(hi_rdy, 2)
            for part in range(3):
                split_lo(0, part)

            dve.wait_ge(lg_mm, 1)
            link(nc.vector.tensor_tensor(lg[:], ps[:, 4, 0:NT * E].rearrange("p (t e) -> p t e", t=NT),
                                         rowb[:, 2 * D:2 * D + E].unsqueeze(1).to_broadcast([P, NT, E]), ALU.add))
            cand = lg[:].unsqueeze(2).to_broadcast([P, NT, E, E])
            for e in range(E):
                me = lg[:, :, e:e + 1]
                if e:
                    own(nc.vector.tensor_tensor(lgt[:, :, e, 0:e], lg[:, :, 0:e], me.to_broadcast([P, NT, e]),
                                                ALU.is_ge))
                own(nc.vector.tensor_tensor(lgt[:, :, e, e:E], lg[:, :, e:E], me.to_broadcast([P, NT, E - e]),
                                            ALU.is_gt))
            own(nc.vector.tensor_reduce(sc[:, 0, :], lg[:], AX.X, ALU.max))
            dve.wait_ge(v_done, n)
            own(nc.vector.tensor_reduce(rk[:], lgt[:], AX.X, ALU.add))
            nc.vector.tensor_tensor(lg[:], lg[:], sc[:, 0, :].unsqueeze(2).to_broadcast([P, NT, E]),
                                    ALU.subtract).then_inc(lg_max, 1)
            dve.wait_ge(v_mm, 1)
            nc.vector.tensor_copy(vm[:].rearrange("p (h n) -> p h n", h=2), ps[0:64, 2:4, 0:HT]).then_inc(v_ev, 1)
            dve.wait_ge(v_done, n)
            dve.wait_ge(lg_exp, 1)
            link(nc.vector.scalar_tensor_tensor(out=comb[:], in0=rk[:], scalar=1.5, in1=comb[:],
                                                op0=ALU.is_lt, op1=ALU.mult))
            link(nc.vector.tensor_reduce(sc[:, 1, :], comb[:], AX.X, ALU.add))
            link(nc.vector.reciprocal(sc[:, 2, :], sc[:, 1, :]))
            link(nc.vector.tensor_tensor(comb[:], comb[:], sc[:, 2, :].unsqueeze(2).to_broadcast([P, NT, E]), ALU.mult))
            link(nc.vector.tensor_copy(comb2[:, :, 0:E], comb[:]))
            link(nc.vector.tensor_tensor(comb2[:, :, E:], comb[:], comb2[:, :, 0:E].bitcast(F32), ALU.subtract))
            nc.vector.tensor_copy(comb2f[:], comb2[:].bitcast(F32)).then_inc(comb_rdy, 1)
            dve.wait_ge(d_misc, 48)
            link(nc.vector.tensor_copy(selr[:], sel_s[:]))
            dve.wait_ge(combt_mm, 1)
            own(nc.vector.tensor_copy(combtf[:], psf[0:2 * E, 6 * 512:6 * 512 + NT * P]))
            dve.wait_ge(v_done, n)
            nc.vector.tensor_copy(combt[:], combtf[:]).then_inc(combt_rdy, 1)

            dve.wait_ge(v_ev, 1)
            for r, c0 in ((slice(0, 32), 0), (slice(32, 64), 32)):
                own(nc.vector.tensor_tensor(vm[r, :].rearrange("p (n b) -> p n b", b=B),
                                            vm[r, :].rearrange("p (n b) -> p n b", b=B),
                                            id_s[r, c0:c0 + B].unsqueeze(1).to_broadcast([32, SEQ, B]), ALU.mult))
            dve.wait_ge(v_done, n)
            v3 = vm[:].rearrange("p (n b) -> p n b", b=B)
            own(nc.vector.tensor_reduce(vseq[0:32, 1:SEQ], v3[0:32, 0:SEQ - 1, :], AX.X, ALU.add))
            own(nc.vector.tensor_reduce(vseq[0:32, 0:1], v3[0:32, SEQ - 1:SEQ, :], AX.X, ALU.add))
            own(nc.vector.tensor_reduce(vseq[32:64, SEQ - 2::-1], v3[32:64, 0:SEQ - 1, :], AX.X, ALU.add))
            own(nc.vector.tensor_reduce(vseq[32:64, SEQ - 1:SEQ], v3[32:64, SEQ - 1:SEQ, :], AX.X, ALU.add))
            dve.wait_ge(v_done, n)
            link(nc.vector.tensor_scalar(vseq[:], vseq[:], vcol("v_b", 0, slice(0, 64)), 3.0, ALU.add, ALU.min))
            link(nc.vector.tensor_scalar(vseq[:], vseq[:], -3.0, -2.0, ALU.max, ALU.add))
            nc.vector.tensor_copy(ar[:, :, 1], vseq[:]).then_inc(vseq_rdy, 1)
            nc.vector.tensor_scalar(ar[:, :, 0], vseq[:], -1.0, None, ALU.mult).then_inc(vseq_rdy, 1)
            dve.wait_ge(d_ffn, 96)
            for f in range(2):
                r = slice(32 * f, 32 * f + B)
                nc.vector.tensor_tensor(ow[r, 0:D], ow[r, 0:D], bkr[r, :], ALU.mult).then_inc(ow_rdy, 1)

            for e in range(1, E, 2):
                dve.wait_ge(cb_mm, e + 1)
                nc.vector.tensor_copy(cb[:, e, :].rearrange("p (h n) -> p h n", h=2), ps[:, 6:8, 0:HT]).then_inc(cb_odd, 1)
            dve.wait_ge(cb_odd, E // 2)
            dve.wait_ge(cb_even, E // 2)

            def hidden(i, j, k):
                s = i * 2 * FK + (j * FK + k)
                sl = j * FK + k
                dve.wait_ge(h_read, s + 3)
                nc.vector.tensor_tensor(hw[:, sl % 2, :], hg[:, sl % 2, :], cb[:, bass.ds(i * 2 + j, 1), :],
                                        ALU.mult).then_inc(hw_rdy, 1)
                dve.wait_ge(hw_rdy, s + 1)
                dve.wait_ge(hh_rdy, s + 1)
                nc.vector.tensor_tensor(hl[:, sl % RING, :], hw[:, sl % 2, :], hh[:, sl % RING, :].bitcast(F32),
                                        ALU.subtract).then_inc(hl_rdy, 1)

            def pair_of_experts(i, last):
                for j in range(2):
                    for k in range(FK):
                        hidden(i, j, k)
                        if not (last and j == 1) and k in (2, 4, 5):
                            part = {2: 0, 4: 1, 5: 2}[k]
                            dve.wait_ge(hi_rdy, i * 4 + (2 * (j + 1) + (1 if part == 0 else 2)))
                            split_lo(1 - j, part)

            with dve.Fori(0, E // 2 - 1) as i:
                pair_of_experts(i, False)
            dve.wait_ge(bk_w, 1)
            nc.vector.reciprocal(wi[:, 5:6], wi[:, 4:5]).then_inc(bk_inv, 1)
            pair_of_experts(E // 2 - 1, True)

            dve.wait_ge(yt_mm, 1)
            for t, r in full[:-1] + [(q, slice(0, TOK - q * P))]:
                bank, off = t // 2, (t % 2) * D
                own(nc.vector.tensor_tensor(zt[r, t, :], ps[r, bank, off:off + D], ht[r, t, 0:D], ALU.add))
            dve.wait_ge(v_done, n)
            norm_stats(lambda t, r: zt[r, t, :], full)
            dve.wait_ge(rstd_rdy, 3)
            for t, r in full:
                nc.vector.tensor_scalar(zt[r, t, :], zt[r, t, :], mv[r, t, 0:1], rstd[r, t:t + 1],
                                        ALU.subtract, ALU.mult).then_inc(fin_rdy, 1)

        @block.tensor
        def _(pe):
            mm = nc.tensor.matmul
            pe.wait_ge(d_had, 32)
            for pt in range(2):
                b = 6 if pt == 0 else 4
                for bank, cs in ((b, slice(0, 2 * D)), (b + 1, slice(2 * D, 3 * D))):
                    for k in range(2):
                        last = mm(ps[:, bank, 0:cs.stop - cs.start], had_s[:, k, pt * P:(pt + 1) * P],
                                  w1t_s[:, k, cs], start=(k == 0), stop=(k == 1))
                last.then_inc(had_mm, 1)
            pe.wait_ge(had_cp, 4)
            pe.wait_ge(d_plw, 16 * KT)
            for k in range(KT):
                pe.wait_ge(d_x[k], 16)
                for m in range(3):
                    for h in range(2):
                        last = mm(ps[:, 2 * m + h, 0:HPX], embed[:, k, m * P:(m + 1) * P],
                                  x_s[:, k, h * HPX:(h + 1) * HPX], start=(k == 0), stop=(k == KT - 1))
            last.then_inc(emb_mm, 1)

            def pointwise(conv, src, bank, kb, ka_tile, kb_tile, m, orows):
                for h in range(2):
                    c = slice(h * HPX, (h + 1) * HPX)
                    mm(ps[orows, bank + h, 0:HPX], pw_s[:, conv, 0, m], src[:, ka_tile, c], start=True, stop=False)
                    last = mm(ps[orows, bank + h, 0:HPX], pw_s[kb, conv, 1, m], src[kb, kb_tile, c],
                              start=False, stop=True)
                return last

            MA, MB = slice(0, P), slice(P, D)
            pe.wait_ge(d_pw, 16)
            pe.wait_ge(dw_done, 3)
            pointwise(1, act_b, 2, HI, 2, 1, MA, A)
            pointwise(1, act_b, 0, HI, 2, 1, MB, HI).then_inc(pw_mm, 1)
            pointwise(0, act_b, 6, LO, 0, 1, MA, A)
            pointwise(0, act_b, 0, LO, 0, 1, MB, LO).then_inc(pw_mm, 1)
            pe.wait_ge(pw_ev, 4)
            pointwise(2, loc, 4, HI, 2, 1, MA, A)
            pointwise(2, loc, 6, HI, 2, 1, MB, LO).then_inc(pw_mm, 1)
            for f in range(3):
                b = 4 if f == 1 else 0
                src = act_b if f == 0 else act_a
                pe.wait_ge(dw_done, 3 + 2 * (f + 1))
                pointwise(3 + f, src, b, LO, 0, 1, MA, A)
                pointwise(3 + f, src, b + 2, LO, 0, 1, MB, LO).then_inc(pw_mm, 1)
            pe.wait_ge(d_proj, 32)
            pe.wait_ge(zeroed, 3)
            pe.wait_ge(pw_ev, 10)
            mm(ps[:, 5, 0:D], zero[:], proj_s[:, 0, :], start=True, stop=False)
            mm(ps[:, 5, 0:D], zero[LO, :], proj_s[LO, 1, :], start=False, stop=False)
            mm(ps[:, 5, 0:D], ones[:], projb_s[:], start=False, stop=True).then_inc(attn_mm, 1)
            pe.wait_ge(d_misc, 48)
            pe.wait_ge(pw_ev, 12)
            for t in range(NT):
                c = slice(t * P, min((t + 1) * P, NPX))
                w = c.stop - c.start
                nc.tensor.transpose(ps[0:w, t, 0:P], act_b[:, 0, c], id_s[:])
                last = nc.tensor.transpose(ps[0:w, t, P:D], act_b[LO, 1, c], id_s[LO, 0:DB])
            last.then_inc(tok_mm, 1)
            for t in range(NT):
                pe.wait_ge(ht_rdy, 2 * t + 2)
                last = nc.tensor.transpose(psf[:, 6 * 512 + t * P:6 * 512 + (t + 1) * P], ht[:, t, 0:P], id_s[:])
            last.then_inc(xt_mm, 1)
            for t in range(NT):
                last = nc.tensor.transpose(psf[:, t * P:(t + 1) * P], ht[:, t, P:256], id_s[:])
            last.then_inc(xt_mm, 1)
            pe.wait_ge(xf_rdy, 2)
            for t in range(NT):
                c = slice(t * P, (t + 1) * P)
                gw = V["gate_w"]
                mm(ps[:, 4, t * E:(t + 1) * E], xf[:, 0, c], vecs[:, gw:gw + E], start=True, stop=False)
                last = mm(ps[:, 4, t * E:(t + 1) * E], xf[LO, 1, c], vecs[LO, gw + E:gw + 2 * E],
                          start=False, stop=True)
            last.then_inc(lg_mm, 1)
            for h in range(2):
                c = slice(h * HT, (h + 1) * HT)
                mm(ps[0:64, 2 + h, 0:HT], vw64[:, 0, :], xf[:, 0, c], start=True, stop=False)
                last = mm(ps[0:64, 2 + h, 0:HT], vw64[LO, 1, :], xf[LO, 1, c], start=False, stop=True)
            last.then_inc(v_mm, 1)
            pe.sem_inc(l2_mm, RING)

            def first_product(slot, k, hs):
                f = slice(k * P, (k + 1) * P)
                for h in range(2):
                    c = slice(h * HT, (h + 1) * HT)
                    o = ps[:, 2 * hs + h, 0:HT]
                    mm(o, w1h[:, slot, 0, f], xh[:, c], start=True, stop=False)
                    mm(o, w1h[:, slot, 0, f], xl[:, c], start=False, stop=False)
                    mm(o, w1l[:, slot, 0, f], xh[:, c], start=False, stop=False)
                    mm(o, w1h[:, slot, 1, f], xb[:, c], start=False, stop=False)
                    last = mm(o, w1l[LO, slot, 1, f], xb[LO, c], start=False, stop=True)
                return last

            def second_product(slot, k, r):
                for h in range(2):
                    c = slice(h * HT, (h + 1) * HT)
                    oa, ob = ps[:, 4 + h, 0:HT], ps[:, 6 + h, 0:HT]
                    mm(oa, w2s[:, slot, k, 0:P], hh[:, r, c], start=False, stop=False)
                    mm(oa, w2s[:, slot, k, 256:384], hh[:, r, c], start=False, stop=False)
                    mm(ob, w2s[:, slot, k, P:256], hh[:, r, c], start=False, stop=False)
                    mm(oa, w2s[:, slot, k, 0:P], hl[:, r, c], start=False, stop=False)
                    last = mm(ps[LO, 6 + h, 0:HT], w2s[:, slot, k, P:D], hl[:, r, c], start=False, stop=False)
                return last

            pe.wait_ge(xs_rdy, 2)
            pe.wait_ge(lo_rdy, 3)
            first_product(0, 0, 0).then_inc(l1_mm, 1)
            pe.wait_ge(v_ev, 1)
            first_product(0, 1, 1).then_inc(l1_mm, 1)
            pe.wait_ge(comb_rdy, 1)
            for t in range(NT):
                last = nc.tensor.transpose(psf[0:2 * E, 6 * 512 + t * P:6 * 512 + (t + 1) * P], comb2f[:, t, :], id_s[:])
            last.then_inc(combt_mm, 1)
            pe.wait_ge(combt_rdy, 1)
            for e in range(E):
                b = 4 + 2 * (e % 2)
                if e >= 2:
                    pe.wait_ge(cb_odd if e % 2 else cb_even, e // 2)
                for h in range(2):
                    last = mm(ps[:, b + h, 0:HT], selr[:, e * P:(e + 1) * P], combt[:, h * HT:(h + 1) * HT],
                              start=True, stop=True)
                last.then_inc(cb_mm, 1)
            pe.wait_ge(cb_even, E // 2)
            pe.wait_ge(cb_odd, E // 2)
            pe.wait_ge(d_ffn, 96)
            for t in range(2):
                for h in range(2):
                    mm(ps[:, 4 + 2 * t + h, 0:HT], b2_s[:, t * P:(t + 1) * P], combtf[:, h * HT:(h + 1) * HT],
                       start=True, stop=False)

            def pair_of_experts(i, last_pair):
                for j in range(2):
                    for k in range(FK):
                        s = i * 2 * FK + (j * FK + k)
                        sl = j * FK + k
                        pe.wait_ge(hl_rdy, s + 1)
                        second_product(j, k, sl % RING).then_inc(l2_mm, 1)
                        if last_pair and sl + LAG >= 2 * FK:
                            continue
                        k1, slot = (k + LAG) % FK, j if k + LAG < FK else 1 - j
                        if k1 == 0:
                            pe.wait_ge(lo_rdy, i * 6 + 3 * (j + 2))
                        pe.wait_ge(h_read, s + (LAG + 1))
                        first_product(slot, k1, sl % 2).then_inc(l1_mm, 1)

            with pe.Fori(0, E // 2 - 1) as i:
                pair_of_experts(i, False)
            pair_of_experts(E // 2 - 1, True)
            pe.wait_ge(bk_rdy, 4)
            pe.wait_ge(ow_rdy, 2)
            for h in range(2):
                c = slice(h * HT, (h + 1) * HT)
                mm(ps[:, 4 + h, 0:HT], ow[:, 0:P], gm[:, c], start=False, stop=True)
                last = mm(ps[:, 6 + h, 0:HT], ow[:, P:2 * P], gm[:, c], start=False, stop=True)
            last.then_inc(y_mm, 1)
            pe.wait_ge(y_ev, 2)
            for t in range(NT):
                c = slice(t * P, min((t + 1) * P, TOK))
                w = c.stop - c.start
                bank, off = t // 2, (t % 2) * D
                nc.tensor.transpose(ps[0:w, bank, off:off + P], yt[:, 0, c], id_s[:])
                last = mm(ps[0:w, bank, off + P:off + D], yt[:, 1, c], pair_s[:], start=True, stop=True)
            last.then_inc(yt_mm, 1)


def haar_matrix():
    k = np.arange(256)[:, None]
    px = np.arange(256)[None, :]
    r, c = px // 16, px % 16
    s = np.zeros((256, 256), np.int64)
    for lv in range(4):
        band = (k >> (2 * (3 - lv))) & 3
        s += (band >> 1) * ((c >> lv) & 1) + (band & 1) * ((r >> lv) & 1)
    return np.where(s % 2, -0.0625, 0.0625).astype(np.float32)


def kernel(**inputs):
    import concourse.bacc as bacc
    from concourse.bass_utils import run_bass_kernel_spmd

    t = {k.replace("L0_tok_", "").replace("L0_attn_", "").replace("L0_ffn_", "f_"): np.asarray(v)
         for k, v in inputs.items()}
    f32 = np.float32

    def parts(v):
        v = v.reshape(D, -1)
        o = np.zeros((P, 2, v.shape[1]), f32)
        o[:, 0] = v[:P]
        o[:DB, 1] = v[P:]
        return o

    def three(a, g):
        a, g = a.reshape(D, -1), g.reshape(D, -1)
        return np.stack([a[:P], np.concatenate([a[P:], g[P:]]), g[:P]], 1)

    vec = np.zeros((P, NVEC), f32)

    def put(name, v):
        v = v.reshape(P, -1)
        vec[:, V[name]:V[name] + v.shape[1]] = v

    put("dw1", three(t["pl_dw"], t["pg_dw"]))
    put("dwf", np.stack([parts(t[f"f{i}_dw"]) for i in (1, 2, 3)], 1))
    put("bias1", three(t["pl_b"], t["pg_b1"]))
    put("bias2", three(t["pl_pwb"], t["pg_pwb"]))
    put("b_w2", parts(t["pg_b2"]))
    put("alpha", parts(t["alpha"]))
    put("fb", np.stack([parts(t[f"f{i}_pwb"]) for i in (1, 2, 3)], 1))
    put("v_w", parts(t["f_v_w"]))
    put("bk", parts(t["f_bk_scale"]))
    put("out_b", parts(t["f_out_b"]))
    put("gate_w", parts(t["f_gate_w"]))
    put("v_b", np.broadcast_to(t["f_v_b"].reshape(1, 1), (P, 1)))
    put("b1", t["f_b1"].reshape(E, FK, P).transpose(2, 0, 1))

    x = t["x"].reshape(B, CIN, G, PATCH, G, PATCH).transpose(1, 3, 5, 2, 4, 0).reshape(KT, P, NPX)
    plw = t["pl_w"].reshape(D, KP).T.reshape(KT, P, D)
    w1t = t["pg_w1"].reshape(D, 256, CIN)
    w1t = np.concatenate([w1t[P:], w1t[:P]]).transpose(1, 2, 0).reshape(2, P, CIN * D).transpose(1, 0, 2)
    had = haar_matrix().reshape(2, P, 256).transpose(1, 0, 2)
    pw = np.zeros((P, 6, 2, D), f32)
    for i, (name, rows) in enumerate([("pl_pw", 0), ("pg_pw", DB), ("pg_w2", DB), ("f1_pw", 0), ("f2_pw", 0),
                                      ("f3_pw", 0)]):
        w = t[name].reshape(D, D).T
        pw[:, i, 0] = w[:P]
        pw[rows:rows + DB, i, 1] = w[P:]
    projw = np.zeros((P, 3 * D), f32)
    projw[:, :2 * D] = parts(t["proj_w"].T).reshape(P, 2 * D)
    projw[0, 2 * D:] = t["proj_b"]
    rows = np.concatenate([t["ln_g"], t["ln_b"], t["f_gate_b"], t["f_bk_scale"]]).reshape(1, -1)
    ident = np.eye(P, dtype=f32)
    pair = np.concatenate([np.eye(DB, dtype=f32)] * 2)
    sel = np.zeros((2, E, E, P), f32)
    for e in range(E):
        sel[:, e, e] = 1.0
    arrays = {
        "x": x, "vec": vec, "rows": rows, "had": had, "w1t": w1t, "plw": plw, "pw": pw, "projw": projw,
        "cls": t["cls"].reshape(1, D), "ident": ident, "pair": pair, "sel": sel.reshape(2 * E, E * P),
        "w1": t["f_w1"], "w2": t["f_w2"].reshape(E, FK, P, D).transpose(0, 2, 1, 3), "b2": t["f_b2"],
        "outw": t["f_out_w"],
    }
    nc = bacc.Bacc("TRN2", target_bir_lowering=False, num_devices=1)
    arrays = {k: np.ascontiguousarray(v) for k, v in arrays.items()}
    args = {k: nc.dram_tensor("in_" + k, v.shape, mybir.dt.from_np(v.dtype), kind="ExternalInput").ap()
            for k, v in arrays.items()}
    out = nc.dram_tensor("out_tokens", (TOK, D), F32, kind="ExternalOutput").ap()
    tower(nc, out=out, **args)
    r = run_bass_kernel_spmd(nc, [{"in_" + k: v for k, v in arrays.items()}], core_ids=[0])
    got = np.asarray(r.results[0]["out_tokens"])
    px = got[:NPX].reshape(G * G, B, D).transpose(1, 0, 2)
    return np.concatenate([got[NPX:][:, None], px], axis=1)
```

```python
from contextlib import ExitStack

import numpy as np

import concourse.bass as bass
from concourse import mybir

F32 = mybir.dt.float32
F32R = mybir.dt.float32r
ALU = mybir.AluOpType
ACT = mybir.ActivationFunctionType
AX = mybir.AxisListType

P = 128
B, CIN, PATCH, G = 16, 3, 16, 6
NPX = G * G * B
HPX = NPX // 2
HB = B // 2
D = 192
DB = D - P
KP = CIN * PATCH * PATCH
KT = KP // P
TOK = NPX + B
HT = TOK // 2
NT = -(-TOK // P)
LAST = NPX - (NT - 1) * P
SEQ = G * G + 1
E, F = 8, 768
FK = F // P
EPS = 1e-5
LAG = 4
RING = 4
PE_TAPS = [(-1, 0), (-1, -1), (-1, 1)]
PE_HELPS = [(0, 1), (1, 0), (1, 1), (2, 0), (2, 1)]
TAPS = [(0, 0)] + [(dy, dx) for dy in (-1, 0, 1) for dx in (-1, 0, 1) if (dy, dx) != (0, 0)]

V = {}
_n = 0
for _name, _w in [("dw1", 27), ("dwf", 54), ("bias1", 3), ("bias2", 3), ("b_w2", 2), ("alpha", 2), ("fb", 6),
                  ("v_w", 2), ("bk", 2), ("out_b", 2), ("gate_w", 16), ("v_b", 1), ("b1", E * FK)]:
    V[_name] = _n
    _n += _w
NVEC = _n


def tower(nc, x, vec, rows, had, w1t, plw, pw, projw, cls, ident, pair, sel, w1, w2, b2, outw, out):
    with ExitStack() as ctx:
        def sb(name, shape, dt=F32):
            return ctx.enter_context(nc.sbuf_tensor(name, shape, dt))

        def sem(name):
            return ctx.enter_context(nc.semaphore(name))

        ps = ctx.enter_context(nc.psum_tensor("ps", [P, 8, 512], F32))
        psf = ps[:].rearrange("p k n -> p (k n)")

        vecs = sb("vecs", [P, NVEC])
        rowb = sb("rowb", [P, 2 * D + E])
        had_s = sb("had_s", [P, 2, 256])
        w1t_s = sb("w1t_s", [P, 2, CIN * D])
        x_s = sb("x_s", [P, KT, NPX])
        embed = sb("embed", [P, KT, 2 * D])
        pw_s = sb("pw_s", [P, 6, 2, D])
        proj_s = sb("proj_s", [P, 2, D])
        projb_s = sb("projb_s", [1, D])
        id_s = sb("id_s", [P, P])
        pair_s = sb("pair_s", [P, DB])
        sel_s = sb("sel_s", [2 * E, E * P])
        cls_s = sb("cls_s", [P, D])
        conv = sb("conv", [P, 3, 3, NPX])
        act_a, act_b = conv[:, 0], conv[:, 1]
        loc = conv[:, 2]
        glob = sb("glob", [P, 2, NPX])
        gate = sb("gate", [P, 8])
        zt = sb("zt", [P, NT, D])
        ht = sb("ht", [P, NT, 256])
        stats = sb("stats", [P, NT, 6])
        mv = sb("mv", [P, NT, 2])
        var = sb("var", [P, NT])
        rstd = sb("rstd", [P, NT])
        neghalf = sb("neghalf", [P, NT + 1])
        zero = sb("zero", [P, P])
        ones = sb("ones", [1, P])
        zeror = sb("zeror", [2 * E, P], F32R)
        attn = sb("attn", [P, D])
        xf = sb("xf", [P, 2, NT * P])
        xh = sb("xh", [P, TOK], F32R)
        xl = sb("xl", [P, TOK], F32R)
        xb = sb("xb", [P, TOK], F32R)
        lg = sb("lg", [P, NT, E])
        lgt = sb("lgt", [P, NT, E, E])
        lge = sb("lge", [P, NT, E, E])
        rk = sb("rk", [P, NT, E])
        sc = sb("sc", [P, 4, NT])
        comb = sb("comb", [P, NT, E])
        comb2 = sb("comb2", [P, NT, 2 * E], F32R)
        combt = sb("combt", [2 * E, NT * P], F32R)
        selr = sb("selr", [2 * E, E * P], F32R)
        cb = conv[:].rearrange("p a t c -> p (a t c)")[:, 0:E * TOK].rearrange("p (e c) -> p e c", e=E)
        vw64 = sb("vw64", [P, 2, 64])
        w1raw = sb("w1raw", [P, 2, 2, F])
        w2raw = sb("w2raw", [P, 2, FK, D])
        diag1 = w1raw[:, 1].rearrange("p a f -> p (a f)")[:, 0:9 * P].rearrange("p (t m k) -> p t m k", t=3, m=3)
        w1h = sb("w1h", [P, 2, 2, F], F32R)
        w1l = sb("w1l", [P, 2, 2, F], F32R)
        w2s = sb("w2s", [P, 2, FK, 2 * D], F32R)
        hgw = sb("hgw", [P, 4, TOK])
        hg, hw = hgw[:, 0:2], hgw[:, 2:4]
        diag = hgw[:].rearrange("p a c -> p (a c)")[:, 0:18 * P].rearrange("p (f t m k) -> p f t m k", f=3, t=2, m=3)
        hh = sb("hh", [P, RING, TOK], F32R)
        hl = sb("hl", [P, RING, TOK], F32R)
        xbh = hh[:, RING - 1]
        yt = x_s[:].rearrange("p k c -> p (k c)")[:, 0:2 * TOK].rearrange("p (t c) -> p t c", t=2)
        vm = x_s[:].rearrange("p k c -> p (k c)")[0:64, 3 * TOK:4 * TOK]
        vseq = sb("vseq", [64, SEQ])
        ar = sb("ar", [64, SEQ, 2])
        tr = sb("tr", [64, SEQ + 2, 2])
        sw = sb("sw", [64, 2, 2])
        phi = sb("phi", [B, SEQ, 2])
        zz = sb("zz", [B, 6, SEQ])
        wi = sb("wi", [B, 8])
        ft = sb("ft", [B, 2, SEQ])
        gm = x_s[:].rearrange("p k c -> p (k c)")[0:80, 2 * TOK:3 * TOK]
        ow = sb("ow", [80, 2 * P])
        bkr = sb("bkr", [48, D])

        d_id = sem("ld_id")
        d_had, d_vec, d_plw, d_pw, d_misc, d_proj, d_ffn, d_cls, d_rows = [
            sem("ld_" + n) for n in ("had", "vec", "plw", "pw", "misc", "proj", "ffn", "cls", "rows")]
        d_x = [sem(f"ld_x{k}") for k in range(4)]
        d_w = [sem("ld_w0"), sem("ld_w1")]
        d_out = sem("stored")
        diag_rdy = sem("diag_rdy")
        tap_mm = sem("tap_mm")
        had_mm = sem("had_mm")
        had_cp = sem("had_cp")
        emb_mm = sem("emb_mm")
        gelu1 = sem("gelu1")
        dw_done = sem("dw_done")
        pw_mm = sem("pw_mm")
        pw_ev = sem("pw_ev")
        gates = sem("gates")
        mixed = sem("mixed")
        v_done = sem("v_done")
        a_done = sem("a_done")
        p_done = sem("p_done")
        zeroed = sem("zeroed")
        attn_mm = sem("attn_mm")
        attn_rdy = sem("attn_rdy")
        tok_mm = sem("tok_mm")
        var_rdy = sem("var_rdy")
        rstd_rdy = sem("rstd_rdy")
        ht_rdy = sem("ht_rdy")
        xt_mm = sem("xt_mm")
        xf_rdy = sem("xf_rdy")
        xa_rdy = sem("xa_rdy")
        xs_rdy = sem("xs_rdy")
        lg_mm = sem("lg_mm")
        lg_max = sem("lg_max")
        lg_exp = sem("lg_exp")
        comb_rdy = sem("comb_rdy")
        combt_mm = sem("combt_mm")
        combt_rdy = sem("combt_rdy")
        v_mm = sem("v_mm")
        v_ev = sem("v_ev")
        vseq_rdy = sem("vseq_rdy")
        cb_mm = sem("cb_mm")
        cb_even = sem("cb_even")
        cb_odd = sem("cb_odd")
        hi1 = sem("hi1")
        hi2 = sem("hi2")
        lo1 = sem("lo1")
        lo2 = sem("lo2")
        l1_mm = sem("l1_mm")
        h_read = sem("h_read")
        hw_rdy = sem("hw_rdy")
        hh_rdy = sem("hh_rdy")
        hl_rdy = sem("hl_rdy")
        l2_mm = sem("l2_mm")
        bk_rdy = sem("bk_rdy")
        ow_zero = sem("ow_zero")
        ow_rdy = sem("ow_rdy")
        y_mm = sem("y_mm")
        y_ev = sem("y_ev")
        yt_mm = sem("yt_mm")
        fin_rdy = sem("fin_rdy")

        def vcol(name, i=0, rows=slice(0, P)):
            return vecs[rows, V[name] + i:V[name] + i + 1]

        A, LO, HI = slice(0, P), slice(0, DB), slice(DB, P)

        block = ctx.enter_context(nc.Block())

        def load_expert(q, e, slot):
            q.dma_start(w1raw[:, slot, 0, :], w1[e, 0:P, :]).then_inc(d_w[slot], 16)
            q.dma_start(w1raw[LO, slot, 1, :], w1[e, P:D, :]).then_inc(d_w[slot], 16)
            q.dma_start(w1raw[HI, slot, 1, :], w1[e, P:D, :]).then_inc(d_w[slot], 16)
            q.dma_start(w2raw[:, slot, :, :], w2[e]).then_inc(d_w[slot], 16)

        @block.sync
        def _(sp):
            sp.dma_start(had_s[:], had).then_inc(d_had, 16)
            sp.dma_start(embed[:, :, 0:D], plw).then_inc(d_plw, 16)
            for g in range(2):
                for kh in range(2):
                    ks = slice(kh * KT // 2, (kh + 1) * KT // 2)
                    sp.dma_start(x_s[:, ks, g * HPX:(g + 1) * HPX], x[g, :, ks, :]).then_inc(d_x[2 * g + kh], 16)
            sp.dma_start(pw_s[:], pw).then_inc(d_pw, 16)
            sp.dma_start(pair_s[:], pair).then_inc(d_misc, 16)
            sp.dma_start(sel_s[:], sel).then_inc(d_misc, 16)
            load_expert(sp, 0, 0)
            sp.wait_ge(tap_mm, 3)
            load_expert(sp, 1, 1)
            for e in range(2, E):
                sp.wait_ge(lo1, e - 1)
                sp.wait_ge(lo2, 2 * (e - 1))
                load_expert(sp, e, e % 2)
            for t in (0, 2, NT - 1):
                sp.wait_ge(fin_rdy, t + 1)
                w = min(P, TOK - P * t)
                sp.dma_start(out[t * P:t * P + w, :], zt[0:w, t, :]).then_inc(d_out, 16)
            sp.wait_ge(d_out, 16 * NT)

        def spectral(pool):
            n = 4
            pool.wait_ge(vseq_rdy, 2)
            nc.gpsimd.memset(gm, 0.0).then_inc(p_done, 1)
            n += 1
            pool.wait_ge(p_done, n)
            for i in range(SEQ):
                nc.gpsimd.tensor_tensor(sw[:, 0, :], tr[:, i, :], tr[:, i + 1, :], ALU.add).then_inc(p_done, 1)
                nc.gpsimd.tensor_tensor(sw[:, 1, :], ar[:, i, :], tr[:, i + 1, ::-1], ALU.mult).then_inc(p_done, 1)
                n += 2
                pool.wait_ge(p_done, n)
                nc.gpsimd.tensor_tensor(tr[:, i + 2, :], sw[:, 0, :], sw[:, 1, :], ALU.add).then_inc(p_done, 1)
                n += 1
                pool.wait_ge(p_done, n)

            def link(ins):
                nonlocal n
                ins.then_inc(p_done, 1)
                n += 1
                pool.wait_ge(p_done, n)

            link(nc.gpsimd.tensor_scalar(wi[:, 0:2], tr[0:B, SEQ + 1, :], 2.0 ** -60, None, ALU.mult))
            link(nc.gpsimd.tensor_tensor(wi[:, 2:4], wi[:, 0:2], wi[:, 0:2], ALU.mult))
            link(nc.gpsimd.tensor_tensor(wi[:, 4:5], wi[:, 2:3], wi[:, 3:4], ALU.add))
            link(nc.gpsimd.tensor_tensor(wi[:, 5:6], wi[:, 4:5], neghalf[0:B, NT:NT + 1], ALU.pow))
            link(nc.gpsimd.tensor_copy(phi[:], tr[32:32 + B, SEQ:0:-1, :]))
            th = tr[0:B, 1:SEQ + 1, :]
            link(nc.gpsimd.tensor_tensor(zz[:, 0, :], th[:, :, 0], phi[:, :, 0], ALU.mult))
            link(nc.gpsimd.tensor_tensor(zz[:, 1, :], th[:, :, 1], phi[:, :, 1], ALU.mult))
            link(nc.gpsimd.tensor_tensor(zz[:, 2, :], th[:, :, 0], phi[:, :, 1], ALU.mult))
            link(nc.gpsimd.tensor_tensor(zz[:, 3, :], th[:, :, 1], phi[:, :, 0], ALU.mult))
            link(nc.gpsimd.tensor_tensor(zz[:, 0, :], zz[:, 0, :], zz[:, 1, :], ALU.subtract))
            link(nc.gpsimd.tensor_tensor(zz[:, 1, :], zz[:, 2, :], zz[:, 3, :], ALU.add))
            link(nc.gpsimd.tensor_scalar(wi[:, 6:8], wi[:, 0:2], wi[:, 5:6], 2.0 ** -60, ALU.mult, ALU.mult))
            link(nc.gpsimd.tensor_scalar(zz[:, 2, :], zz[:, 0, :], wi[:, 6:7], None, ALU.mult))
            link(nc.gpsimd.tensor_scalar(zz[:, 3, :], zz[:, 1, :], wi[:, 7:8], None, ALU.mult))
            link(nc.gpsimd.tensor_scalar(zz[:, 4, :], zz[:, 1, :], wi[:, 6:7], None, ALU.mult))
            link(nc.gpsimd.tensor_scalar(zz[:, 5, :], zz[:, 0, :], wi[:, 7:8], None, ALU.mult))
            link(nc.gpsimd.tensor_tensor(ft[:, 0, :], zz[:, 5, :], zz[:, 4, :], ALU.subtract))
            link(nc.gpsimd.tensor_tensor(ft[:, 1, :], zz[:, 2, :], zz[:, 3, :], ALU.add))
            nc.gpsimd.tensor_copy(gm[64:64 + 2 * E, :], combt[:, 0:TOK].bitcast(F32)).then_inc(bk_rdy, 1)
            link(nc.gpsimd.tensor_scalar(ft[:], ft[:], 10.0, -10.0, ALU.min, ALU.max))
            for f in range(2):
                r = slice(32 * f, 32 * f + B)
                mask = id_s[0:B, 0:B]
                for g in range(2):
                    nc.gpsimd.tensor_tensor(
                        gm[r, g * HPX:(g + 1) * HPX].rearrange("p (n b) -> p n b", b=HB),
                        ft[:, f, 1:SEQ].unsqueeze(2).to_broadcast([B, SEQ - 1, HB]),
                        mask[:, g * HB:(g + 1) * HB].unsqueeze(1).to_broadcast([B, SEQ - 1, HB]),
                        ALU.mult).then_inc(bk_rdy, 1)
                nc.gpsimd.tensor_tensor(gm[r, NPX:TOK], ft[:, f, 0:1].to_broadcast([B, B]), mask,
                                        ALU.mult).then_inc(bk_rdy, 1)

        @block.gpsimd
        def _(pool):
            nc.gpsimd.memset(neghalf[:, 0:NT], -0.5).then_inc(p_done, 1)
            nc.gpsimd.memset(neghalf[:, NT:], -1.0).then_inc(p_done, 1)
            nc.gpsimd.memset(tr[:], 0.0).then_inc(p_done, 1)
            nc.gpsimd.memset(ow[:], 0.0).then_inc(ow_zero, 1)
            pool.wait_ge(p_done, 3)
            nc.gpsimd.memset(tr[:, 1:2, 0:1], 1.0).then_inc(p_done, 1)
            pool.wait_ge(d_vec, 16)
            pool.wait_ge(d_id, 16)
            for t in range(3):
                for m, (dy, dx) in enumerate(PE_TAPS):
                    tap = V["dw1"] + 9 * t + (dy + 1) * 3 + dx + 1
                    nc.gpsimd.tensor_scalar(diag1[:, t, m, :], id_s[:], vecs[:, tap:tap + 1], None,
                                            ALU.mult).then_inc(diag_rdy, 1)
            for f in range(3):
                for t in range(2):
                    for m, (dy, dx) in enumerate(PE_TAPS):
                        tap = V["dwf"] + 18 * f + 9 * t + (dy + 1) * 3 + dx + 1
                        nc.gpsimd.tensor_scalar(diag[:, f, t, m, :], id_s[:], vecs[:, tap:tap + 1], None,
                                                ALU.mult).then_inc(diag_rdy, 1)
            for k, ts in enumerate((slice(0, 2), slice(2, NT), slice(0, NT), slice(0, 2), slice(2, NT))):
                pool.wait_ge(var_rdy, k + 1)
                nc.gpsimd.tensor_tensor(rstd[:, ts], var[:, ts], neghalf[:, ts], ALU.pow).then_inc(rstd_rdy, 1)
                if k == 2:
                    spectral(pool)

        @block.scalar
        def _(act):
            act.dma_start(w1t_s[:], w1t).then_inc(d_had, 16)
            act.dma_start(vecs[:], vec).then_inc(d_vec, 16)
            act.dma_start(id_s[:], ident).then_inc(d_id, 16)
            act.dma_start(proj_s[:], projw[:, 0:2 * D].rearrange("p (t d) -> p t d", t=2)).then_inc(d_proj, 16)
            act.dma_start(projb_s[:], projw[0:1, 2 * D:3 * D]).then_inc(d_proj, 16)
            act.dma_start(cls_s[LAST:LAST + B, :], cls.to_broadcast([B, D])).then_inc(d_cls, 16)
            act.dma_start(rowb[:], rows[0:1, 0:2 * D + E].to_broadcast([P, 2 * D + E])).then_inc(d_rows, 16)
            act.wait_ge(ow_zero, 1)
            for f in range(2):
                act.dma_start(ow[32 * f:32 * f + B, 0:D], outw[f:f + 1, :].to_broadcast([B, D])).then_inc(d_ffn, 16)
                act.dma_start(bkr[32 * f:32 * f + B, :],
                              rows[0:1, 2 * D + E:3 * D + E].to_broadcast([B, D])).then_inc(d_ffn, 16)
                act.dma_start(ow[64 + E * f:64 + E * f + E, 0:D], b2).then_inc(d_ffn, 16)
            act.wait_ge(d_vec, 16)
            nc.scalar.activation(gate[:, 0:2], vecs[:, V["alpha"]:V["alpha"] + 2], ACT.Tanh).then_inc(a_done, 1)
            for pt in range(2):
                act.wait_ge(had_mm, pt + 1)
                b = 4 + 2 * pt
                nc.scalar.copy(embed[:, pt:pt + 3:2, D:2 * D],
                               ps[:, b, 0:2 * D].rearrange("p (c n) -> p c n", c=2)).then_inc(had_cp, 1)
                nc.scalar.copy(embed[:, 4 + pt, D:2 * D], ps[:, b + 1, 0:D]).then_inc(had_cp, 1)

            def px(g):
                return slice(g * HPX, (g + 1) * HPX)

            def embed_out(g):
                for t in range(3):
                    act.wait_ge(emb_mm, 3 * g + t + 1)
                    nc.scalar.activation(act_a[:, t, px(g)], ps[:, 4 * g + t, 0:HPX], ACT.Gelu,
                                         bias=vcol("bias1", t)).then_inc(gelu1, 1)

            def evacuate(n, bank, dst, rows_, func, bias, scale=1.0):
                act.wait_ge(pw_mm, n)
                nc.scalar.activation(dst, ps[rows_, bank, 0:HPX], func, bias=bias, scale=scale).then_inc(pw_ev, 1)

            def branches(g):
                b, n = 4 * g, 6 * g
                evacuate(n + 1, b + 2, loc[:, 2, px(g)], A, ACT.Gelu, vcol("bias2", 2))
                evacuate(n + 2, b + 1, loc[HI, 1, px(g)], HI, ACT.Gelu, vcol("bias2", 1, HI))
                evacuate(n + 3, b, loc[:, 0, px(g)], A, ACT.Identity, vcol("bias2", 0))
                evacuate(n + 4, b + 1, loc[LO, 1, px(g)], LO, ACT.Identity, vcol("bias2", 1, LO))
                if g == 0:
                    act.wait_ge(gates, 1)
                evacuate(n + 5, b + 2, glob[:, 0, px(g)], A, ACT.Identity, gate[:, 6:7], gate[:, 2:3])
                evacuate(n + 6, b + 3, glob[LO, 1, px(g)], LO, ACT.Identity, gate[LO, 7:8], gate[LO, 3:4])

            def fusion(f, g):
                n, b = 12 + 4 * f + 2 * g, 4 * g
                fn = ACT.Relu if f < 2 else ACT.Identity
                evacuate(n + 1, b, act_a[:, 0, px(g)], A, fn, vcol("fb", 2 * f))
                evacuate(n + 2, b + 1, act_a[LO, 1, px(g)], LO, fn, vcol("fb", 2 * f + 1, LO))

            def split_hi1(slot):
                nc.scalar.copy(w1h[:, slot, :, :], w1raw[:, slot, :, :]).then_inc(hi1, 1)

            def split_hi2(slot):
                nc.scalar.copy(w2s[:, slot, :, 0:D], w2raw[:, slot, :, :]).then_inc(hi2, 1)

            embed_out(0)
            embed_out(1)
            act.wait_ge(attn_mm, 1)
            nc.scalar.copy(attn[:], ps[:, 3, 0:D]).then_inc(attn_rdy, 1)
            branches(0)
            branches(1)
            for f in range(3):
                for g in range(2):
                    fusion(f, g)
                    if (f, g) == (1, 0):
                        act.wait_ge(d_w[0], 64)
                        split_hi1(0)
                        split_hi2(0)

            act.wait_ge(xt_mm, 1)
            nc.scalar.copy(xf[:, 0, :], psf[:, 6 * 512:6 * 512 + NT * P]).then_inc(xa_rdy, 1)
            act.wait_ge(xa_rdy, 1)
            nc.scalar.copy(xh[:], xf[:, 0, 0:TOK]).then_inc(xa_rdy, 1)
            act.wait_ge(xf_rdy, 1)
            nc.scalar.copy(xb[LO, :], xf[LO, 1, 0:TOK]).then_inc(xs_rdy, 1)
            nc.scalar.sem_inc(h_read, 2)
            act.wait_ge(lg_max, 1)
            nc.scalar.activation(comb[:], lg[:], ACT.Exp).then_inc(lg_exp, 1)

            def gelu(i, sl):
                act.wait_ge(l1_mm, i * 2 * FK + (sl + 1))
                nc.scalar.activation(hg[:, sl % 2, :].rearrange("p (h n) -> p h n", h=2),
                                     ps[:, 2 * (sl % 2):2 * (sl % 2) + 2, 0:HT], ACT.Gelu_apprx_tanh,
                                     bias=vecs[:, bass.ds(i * 2 * FK + (V["b1"] + sl), 1)]).then_inc(h_read, 1)

            def pair_of_experts(i, last):
                for sl in range(2 * FK):
                    j, k = divmod(sl, FK)
                    s = i * 2 * FK + sl
                    act.wait_ge(hw_rdy, s + 1)
                    act.wait_ge(l2_mm, s + 1)
                    nc.scalar.copy(hh[:, sl % RING, :], hw[:, sl % 2, :]).then_inc(hh_rdy, 1)
                    if not (last and sl >= 2 * FK - 2):
                        gelu(i, sl + 2)
                    if last and j == 1:
                        continue
                    if k == 0:
                        act.wait_ge(d_w[1 - j], (i + 1 + j) * 64)
                        split_hi1(1 - j)
                    if k == 3:
                        act.wait_ge(l2_mm, i * 2 * FK + (j * FK + RING))
                        split_hi2(1 - j)

            gelu(0, 0)
            gelu(0, 1)
            for e in range(0, E, 2):
                act.wait_ge(cb_mm, e + 1)
                nc.scalar.copy(cb[:, e, :].rearrange("p (h n) -> p h n", h=2), ps[:, 4:6, 0:HT]).then_inc(cb_even, 1)
            with act.Fori(0, E // 2 - 1) as i:
                pair_of_experts(i, False)
            pair_of_experts(E // 2 - 1, True)
            act.wait_ge(y_mm, 1)
            for h in range(2):
                for t in range(2):
                    nc.scalar.activation(yt[:, t, h * HT:(h + 1) * HT], ps[:, 4 + 2 * t + h, 0:HT], ACT.Identity,
                                         bias=gate[:, 4 + t:5 + t]).then_inc(y_ev, 1)
            for t in (1, 3):
                act.wait_ge(fin_rdy, t + 1)
                act.dma_start(out[t * P:(t + 1) * P, :], zt[:, t, :]).then_inc(d_out, 16)

        @block.vector
        def _(dve):
            n = 0

            def own(ins):
                nonlocal n
                n += 1
                ins.then_inc(v_done, 1)
                return n

            def link(ins):
                dve.wait_ge(v_done, own(ins))

            nc.vector.memset(zero[:], 0.0).then_inc(zeroed, 1)
            nc.vector.memset(ones[:], 1.0).then_inc(zeroed, 1)
            nc.vector.memset(zeror[:].bitcast(F32), 0.0).then_inc(zeroed, 1)
            link(nc.vector.memset(zt[HI, NT - 1, :], 0.0))
            link(nc.vector.memset(mv[:], 0.0))
            dve.wait_ge(d_vec, 16)
            link(nc.vector.tensor_copy(vw64[:], vecs[:, V["v_w"]:V["v_w"] + 2].unsqueeze(2).to_broadcast([P, 2, 64])))
            link(nc.vector.tensor_tensor(gate[:, 4:6], vecs[:, V["bk"]:V["bk"] + 2], vecs[:, V["out_b"]:V["out_b"] + 2],
                                         ALU.mult))
            dve.wait_ge(a_done, 1)
            link(nc.vector.tensor_scalar(gate[:, 2:4], gate[:, 0:2], 1.0, 0.5, ALU.add, ALU.mult))
            link(nc.vector.tensor_scalar(gate[:, 0:2], gate[:, 2:4], -1.0, 1.0, ALU.mult, ALU.add))
            nc.vector.tensor_tensor(gate[:, 6:8], gate[:, 2:4], vecs[:, V["b_w2"]:V["b_w2"] + 2],
                                    ALU.mult).then_inc(gates, 1)

            def depthwise(src, dst, taps, tiles, g, help_at=None):
                mark = {}

                def rect(buf, rows_, t, dy, dx, sy, sx):
                    y0, y1, x0, x1 = max(0, -dy), G - max(0, dy), max(0, -dx), G - max(0, dx)
                    v = buf[rows_, t, g * HPX:(g + 1) * HPX].rearrange("p (y x) -> p y x", y=G)
                    return v[:, y0 + sy:y1 + sy, (x0 + sx) * HB:(x1 + sx) * HB]

                mine = [tp for tp in TAPS if help_at is None or tp not in PE_TAPS]
                for m, (dy, dx) in enumerate(mine):
                    tap = (dy + 1) * 3 + dx + 1
                    for t, rows_ in tiles:
                        o, a = rect(dst, rows_, t, dy, dx, 0, 0), rect(src, rows_, t, dy, dx, dy, dx)
                        w = vecs[rows_, taps + 9 * t + tap:taps + 9 * t + tap + 1]
                        if m == 0:
                            ins = nc.vector.tensor_scalar(o, a, w, None, ALU.mult)
                        else:
                            dve.wait_ge(v_done, mark[t])
                            ins = nc.vector.scalar_tensor_tensor(out=o, in0=a, scalar=w, in1=o, op0=ALU.mult,
                                                                 op1=ALU.add)
                        if help_at is None and m == len(mine) - 1:
                            ins.then_inc(dw_done, 1)
                        else:
                            mark[t] = own(ins)
                if help_at is not None:
                    for t, rows_ in tiles:
                        dve.wait_ge(tap_mm, help_at + 1)
                        help_at += 1
                        dve.wait_ge(v_done, mark[t])
                        c = slice(g * HPX + G * HB, (g + 1) * HPX)
                        nc.vector.tensor_tensor(dst[rows_, t, c], ps[rows_, (4 * g + t + (0 if len(tiles) == 3 else 2)), G * HB:HPX],
                                                dst[rows_, t, c], ALU.add).then_inc(dw_done, 1)

            def split_lo1(slot):
                nc.vector.tensor_tensor(w1l[:, slot, :, :], w1raw[:, slot, :, :],
                                        w1h[:, slot, :, :].bitcast(F32), ALU.subtract).then_inc(lo1, 1)

            def split_lo2(slot, part):
                a, o = ((slice(P, D), slice(D, 256)), (slice(0, P), slice(256, 2 * D)))[part]
                nc.vector.tensor_tensor(w2s[:, slot, :, o], w2raw[:, slot, :, a],
                                        w2s[:, slot, :, a].bitcast(F32), ALU.subtract).then_inc(lo2, 1)

            two = [(0, A), (1, LO)]
            for g in range(2):
                dve.wait_ge(gelu1, 3 * g + 3)
                depthwise(act_a, act_b, V["dw1"], [(2, A), (1, A), (0, A)], g, 0 if g else None)
            for f in range(3):
                for g in range(2):
                    c = slice(g * HPX, (g + 1) * HPX)
                    if f == 0:
                        dve.wait_ge(pw_ev, 6 * g + 6)
                        for t, rows_ in two:
                            nc.vector.scalar_tensor_tensor(out=act_a[rows_, t, c], in0=loc[rows_, t, c],
                                                           scalar=gate[rows_, t:t + 1], in1=glob[rows_, t, c],
                                                           op0=ALU.mult, op1=ALU.add).then_inc(mixed, 1)
                        dve.wait_ge(mixed, 2 * g + 2)
                    else:
                        dve.wait_ge(pw_ev, 12 + 4 * (f - 1) + 2 * g + 2)
                    if f == 2:
                        for t, rows_ in two:
                            nc.vector.tensor_tensor(glob[rows_, t, c], act_a[rows_, t, c], loc[rows_, t, c],
                                                    ALU.add).then_inc(mixed, 1)
                        dve.wait_ge(mixed, 4 + 2 * g + 2)
                    src, dst = (act_a, act_a, glob)[f], act_b
                    depthwise(src, dst, V["dwf"] + 18 * f, two, g,
                              3 + 2 * PE_HELPS.index((f, g)) if (f, g) in PE_HELPS else None)
            dve.wait_ge(hi1, 1)
            split_lo1(0)
            dve.wait_ge(hi2, 1)
            split_lo2(0, 0)
            split_lo2(0, 1)

            def norm_stats(src, tiles):
                for t, rows_ in tiles:
                    own(nc.vector.bn_stats(stats[rows_, t, :], src(t, rows_)))
                dve.wait_ge(v_done, n)
                for t, rows_ in tiles:
                    own(nc.vector.bn_aggr(mv[rows_, t, :], stats[rows_, t, :]))
                dve.wait_ge(v_done, n)
                ts = slice(tiles[0][0], tiles[-1][0] + 1)
                nc.vector.tensor_scalar(var[:, ts], mv[:, ts, 1], EPS, None, ALU.add).then_inc(var_rdy, 1)

            full = [(t, A) for t in range(NT)]
            cr = slice(LAST, LAST + B)
            last_px = [(NT - 1, slice(0, LAST))]
            dve.wait_ge(d_rows, 16)
            dve.wait_ge(attn_rdy, 1)
            dve.wait_ge(d_cls, 16)
            own(nc.vector.tensor_tensor(rowb[:, D:2 * D], rowb[:, D:2 * D], attn[:], ALU.add))
            own(nc.vector.tensor_tensor(zt[cr, NT - 1, :], cls_s[cr, :], attn[cr, :], ALU.add))

            def first_norm(tiles, k):
                norm_stats(lambda t, r: ps[r, t, 0:D], tiles)
                for t, r in tiles:
                    own(nc.vector.scalar_tensor_tensor(out=zt[r, t, :], in0=ps[r, t, 0:D], scalar=mv[r, t, 0:1],
                                                       in1=rowb[r, 0:D], op0=ALU.subtract, op1=ALU.mult))
                dve.wait_ge(v_done, n)
                dve.wait_ge(rstd_rdy, k)
                for t, r in tiles:
                    own(nc.vector.scalar_tensor_tensor(out=zt[r, t, :], in0=zt[r, t, :], scalar=rstd[r, t:t + 1],
                                                       in1=rowb[r, D:2 * D], op0=ALU.mult, op1=ALU.add))
                dve.wait_ge(v_done, n)

            def second_norm(tiles, k):
                norm_stats(lambda t, r: zt[r, t, :], tiles)
                dve.wait_ge(rstd_rdy, k)
                for t, r in tiles:
                    nc.vector.tensor_scalar(ht[r, t, 0:D], zt[r, t, :], mv[r, t, 0:1], rstd[r, t:t + 1],
                                            ALU.subtract, ALU.mult).then_inc(ht_rdy, 1)
                    nc.vector.tensor_scalar(ht[r, t, D:256], zt[r, t, P:D], mv[r, t, 0:1], rstd[r, t:t + 1],
                                            ALU.subtract, ALU.mult).then_inc(ht_rdy, 1)

            dve.wait_ge(d_misc, 32)
            nc.vector.tensor_copy(selr[:], sel_s[:]).then_inc(zeroed, 1)
            dve.wait_ge(tok_mm, 1)
            first_norm(full[:2], 1)
            dve.wait_ge(tok_mm, 2)
            first_norm(full[2:-1] + last_px, 2)
            second_norm(full, 3)
            dve.wait_ge(xt_mm, 2)
            nc.vector.tensor_copy(xf[:, 1, :], psf[:, 0:NT * P]).then_inc(xf_rdy, 1)
            dve.wait_ge(xf_rdy, 1)
            link(nc.vector.tensor_copy(xbh[HI, :], psf[HI, 0:TOK]))
            nc.vector.tensor_tensor(xb[HI, :], psf[HI, 0:TOK], xbh[HI, :].bitcast(F32),
                                    ALU.subtract).then_inc(xs_rdy, 1)
            dve.wait_ge(xa_rdy, 2)
            nc.vector.tensor_tensor(xl[:], xf[:, 0, 0:TOK], xh[:].bitcast(F32), ALU.subtract).then_inc(xs_rdy, 1)

            def routed(i, sl):
                dve.wait_ge(h_read, i * 2 * FK + (sl + 3))
                if sl:
                    dve.wait_ge(hl_rdy, i * 2 * FK + sl)
                nc.vector.tensor_tensor(hw[:, sl % 2, :], hg[:, sl % 2, :], cb[:, bass.ds(i * 2 + sl // FK, 1), :],
                                        ALU.mult).then_inc(hw_rdy, 1)

            dve.wait_ge(lg_mm, 1)
            link(nc.vector.tensor_tensor(lg[:], ps[:, 4, 0:NT * E].rearrange("p (t e) -> p t e", t=NT),
                                         rowb[:, 2 * D:2 * D + E].unsqueeze(1).to_broadcast([P, NT, E]), ALU.add))
            cand = lg[:].unsqueeze(2).to_broadcast([P, NT, E, E])
            for e in range(E):
                me = lg[:, :, e:e + 1]
                if e:
                    own(nc.vector.tensor_tensor(lgt[:, :, e, 0:e], lg[:, :, 0:e], me.to_broadcast([P, NT, e]),
                                                ALU.is_ge))
                own(nc.vector.tensor_tensor(lgt[:, :, e, e:E], lg[:, :, e:E], me.to_broadcast([P, NT, E - e]),
                                            ALU.is_gt))
            own(nc.vector.tensor_reduce(sc[:, 0, :], lg[:], AX.X, ALU.max))
            dve.wait_ge(v_done, n)
            own(nc.vector.tensor_reduce(rk[:], lgt[:], AX.X, ALU.add))
            nc.vector.tensor_tensor(lg[:], lg[:], sc[:, 0, :].unsqueeze(2).to_broadcast([P, NT, E]),
                                    ALU.subtract).then_inc(lg_max, 1)
            dve.wait_ge(v_mm, 1)
            nc.vector.tensor_copy(vm.rearrange("p (h n) -> p h n", h=2), ps[0:64, 2:4, 0:HT]).then_inc(v_ev, 1)
            dve.wait_ge(v_done, n)
            dve.wait_ge(lg_exp, 1)
            link(nc.vector.scalar_tensor_tensor(out=comb[:], in0=rk[:], scalar=1.5, in1=comb[:],
                                                op0=ALU.is_lt, op1=ALU.mult))
            link(nc.vector.tensor_reduce(sc[:, 1, :], comb[:], AX.X, ALU.add))
            link(nc.vector.reciprocal(sc[:, 2, :], sc[:, 1, :]))
            link(nc.vector.tensor_tensor(comb[:], comb[:], sc[:, 2, :].unsqueeze(2).to_broadcast([P, NT, E]), ALU.mult))
            link(nc.vector.tensor_copy(comb2[:, :, 0:E], comb[:]))
            nc.vector.tensor_tensor(comb2[:, :, E:], comb[:], comb2[:, :, 0:E].bitcast(F32),
                                    ALU.subtract).then_inc(comb_rdy, 1)
            dve.wait_ge(combt_mm, 1)
            nc.vector.tensor_copy(combt[:], psf[0:2 * E, 6 * 512:6 * 512 + NT * P]).then_inc(combt_rdy, 1)
            for e in range(1, E, 2):
                dve.wait_ge(cb_mm, e + 1)
                nc.vector.tensor_copy(cb[:, e, :].rearrange("p (h n) -> p h n", h=2), ps[:, 6:8, 0:HT]).then_inc(cb_odd, 1)
            dve.wait_ge(cb_odd, E // 2)
            dve.wait_ge(cb_even, E // 2)
            routed(0, 0)
            dve.sem_inc(hl_rdy, 1)

            dve.wait_ge(v_ev, 1)
            for r, c0 in ((slice(0, 32), 0), (slice(32, 64), 32)):
                mask = id_s[r, c0:c0 + B]
                own(nc.vector.tensor_tensor(vm[r, 0:NPX].rearrange("p (g n b) -> p g n b", g=2, b=HB),
                                            vm[r, 0:NPX].rearrange("p (g n b) -> p g n b", g=2, b=HB),
                                            mask.rearrange("p (g b) -> p g b", g=2).unsqueeze(2)
                                            .to_broadcast([32, 2, SEQ - 1, HB]), ALU.mult))
                own(nc.vector.tensor_tensor(vm[r, NPX:TOK], vm[r, NPX:TOK], mask, ALU.mult))
            dve.wait_ge(v_done, n)
            v4 = vm[:, 0:NPX].rearrange("p (g n b) -> p n g b", g=2, b=HB)
            own(nc.vector.tensor_reduce(vseq[0:32, 1:SEQ], v4[0:32], AX.XY, ALU.add))
            own(nc.vector.tensor_reduce(vseq[0:32, 0:1], vm[0:32, NPX:TOK], AX.X, ALU.add))
            own(nc.vector.tensor_reduce(vseq[32:64, SEQ - 2::-1], v4[32:64], AX.XY, ALU.add))
            own(nc.vector.tensor_reduce(vseq[32:64, SEQ - 1:SEQ], vm[32:64, NPX:TOK], AX.X, ALU.add))
            dve.wait_ge(v_done, n)
            link(nc.vector.tensor_scalar(vseq[:], vseq[:], vcol("v_b", 0, slice(0, 64)), 3.0, ALU.add, ALU.min))
            link(nc.vector.tensor_scalar(vseq[:], vseq[:], -3.0, -2.0, ALU.max, ALU.add))
            nc.vector.tensor_copy(ar[:, :, 1], vseq[:]).then_inc(vseq_rdy, 1)
            nc.vector.tensor_scalar(ar[:, :, 0], vseq[:], -1.0, None, ALU.mult).then_inc(vseq_rdy, 1)
            dve.wait_ge(d_ffn, 96)
            for f in range(2):
                r = slice(32 * f, 32 * f + B)
                nc.vector.tensor_tensor(ow[r, 0:D], ow[r, 0:D], bkr[r, :], ALU.mult).then_inc(ow_rdy, 1)

            def pair_of_experts(i, last):
                for sl in range(2 * FK):
                    j, k = divmod(sl, FK)
                    s = i * 2 * FK + sl
                    if not (last and sl == 2 * FK - 1):
                        routed(i, sl + 1)
                    dve.wait_ge(hh_rdy, s + 1)
                    nc.vector.tensor_tensor(hl[:, sl % RING, :], hw[:, sl % 2, :], hh[:, sl % RING, :].bitcast(F32),
                                            ALU.subtract).then_inc(hl_rdy, 1)
                    if last and j == 1:
                        continue
                    if k == 1:
                        dve.wait_ge(hi1, i * 2 + (j + 2))
                        split_lo1(1 - j)
                    if k == 4:
                        dve.wait_ge(hi2, i * 2 + (j + 2))
                        split_lo2(1 - j, 0)
                    if k == 5:
                        split_lo2(1 - j, 1)

            with dve.Fori(0, E // 2 - 1) as i:
                pair_of_experts(i, False)
            pair_of_experts(E // 2 - 1, True)

            q = NT - 1

            def residual(tiles):
                for t, r in tiles:
                    bank, off = (0, 2)[t // 2 % 2] + t // 4, (t % 2) * D
                    if t in (0, 2, q):
                        dve.wait_ge(yt_mm, t // 2 + 1)
                    own(nc.vector.tensor_tensor(zt[r, t, :], ps[r, bank, off:off + D], ht[r, t, 0:D], ALU.add))
                dve.wait_ge(v_done, n)

            def last_norm(tiles, k):
                dve.wait_ge(rstd_rdy, k)
                for t, r in tiles:
                    nc.vector.tensor_scalar(zt[r, t, :], zt[r, t, :], mv[r, t, 0:1], rstd[r, t:t + 1],
                                            ALU.subtract, ALU.mult).then_inc(fin_rdy, 1)

            residual(full[:2])
            norm_stats(lambda t, r: zt[r, t, :], full[:2])
            residual(full[2:q] + [(q, slice(0, TOK - q * P))])
            norm_stats(lambda t, r: zt[r, t, :], full[2:])
            last_norm(full[:2], 4)
            last_norm(full[2:], 5)

        @block.tensor
        def _(pe):
            mm = nc.tensor.matmul
            pe.wait_ge(d_had, 32)
            for pt in range(2):
                b = 4 + 2 * pt
                for bank, cs in ((b, slice(0, 2 * D)), (b + 1, slice(2 * D, 3 * D))):
                    for k in range(2):
                        last = mm(ps[:, bank, 0:cs.stop - cs.start], had_s[:, k, pt * P:(pt + 1) * P],
                                  w1t_s[:, k, cs], start=(k == 0), stop=(k == 1))
                last.then_inc(had_mm, 1)

            def embed_half(g):
                for m in range(3):
                    for k in range(KT):
                        if m == 0:
                            pe.wait_ge(d_x[2 * g + k // (KT // 2)], 16)
                        if m == 1 and k == 0 and g == 0:
                            pe.wait_ge(had_cp, 4)
                        last = mm(ps[:, 4 * g + m, 0:HPX], embed[:, k, m * P:(m + 1) * P],
                                  x_s[:, k, g * HPX:(g + 1) * HPX], start=(k == 0), stop=(k == KT - 1))
                    last.then_inc(emb_mm, 1)

            def pointwise(conv_, src, g, bank, kb, ka_tile, m, orows):
                c = slice(g * HPX, (g + 1) * HPX)
                mm(ps[orows, bank, 0:HPX], pw_s[:, conv_, 0, m], src[:, ka_tile, c], start=True, stop=False)
                mm(ps[orows, bank, 0:HPX], pw_s[kb, conv_, 1, m], src[kb, 1, c],
                   start=False, stop=True).then_inc(pw_mm, 1)

            MA, MB = slice(0, P), slice(P, D)

            def branches(g):
                b = 4 * g
                pe.wait_ge(dw_done, 3 * g + 3)
                pointwise(1, act_b, g, b + 2, HI, 2, MA, A)
                pointwise(1, act_b, g, b + 1, HI, 2, MB, HI)
                pointwise(0, act_b, g, b, LO, 0, MA, A)
                pointwise(0, act_b, g, b + 1, LO, 0, MB, LO)
                pe.wait_ge(pw_ev, 6 * g + 2)
                if g == 0:
                    pe.wait_ge(attn_rdy, 1)
                pointwise(2, loc, g, b + 2, HI, 2, MA, A)
                pointwise(2, loc, g, b + 3, HI, 2, MB, LO)

            def fusion(f, g):
                b = 4 * g
                src = act_b
                pe.wait_ge(dw_done, 6 + 4 * f + 2 * g + 2)
                pointwise(3 + f, src, g, b, LO, 0, MA, A)
                pointwise(3 + f, src, g, b + 1, LO, 0, MB, LO)

            def taps(f, g):
                if f == 0:
                    pe.wait_ge(mixed, 2 * g + 2)
                elif f == 1:
                    pe.wait_ge(pw_ev, 12 + 2 * g + 2)
                else:
                    pe.wait_ge(mixed, 4 + 2 * g + 2)
                pe.wait_ge(diag_rdy, 9 + 6 * (f + 1))
                for t, rows_ in ((0, A), (1, LO)):
                    tap_sums((act_a, act_a, glob)[f], g, t, rows_, diag[:, f, t], 4 * g + 2 + t)

            def tap_sums(src, g, t, rows_, mats, bank):
                v = src[rows_, t, g * HPX:(g + 1) * HPX].rearrange("p (y x) -> p y x", y=G)
                o = ps[rows_, bank, 0:HPX].rearrange("p (y x) -> p y x", y=G)
                for m, (dy, dx) in enumerate(PE_TAPS):
                    x0, x1 = max(0, -dx), G - max(0, dx)
                    last = mm(o[:, 1:G, x0 * HB:x1 * HB], mats[rows_, m, 0:rows_.stop],
                              v[:, 0:G - 1, (x0 + dx) * HB:(x1 + dx) * HB],
                              start=(m == 0), stop=(m == len(PE_TAPS) - 1))
                last.then_inc(tap_mm, 1)

            pe.wait_ge(d_plw, 16)
            embed_half(0)
            embed_half(1)
            pe.wait_ge(d_proj, 32)
            pe.wait_ge(zeroed, 3)
            mm(ps[:, 3, 0:D], zero[:], proj_s[:, 0, :], start=True, stop=False)
            mm(ps[:, 3, 0:D], zero[LO, :], proj_s[LO, 1, :], start=False, stop=False)
            mm(ps[:, 3, 0:D], ones[:], projb_s[:], start=False, stop=True).then_inc(attn_mm, 1)
            pe.wait_ge(diag_rdy, 9)
            pe.wait_ge(gelu1, 6)
            for t in (2, 1, 0):
                tap_sums(act_a, 1, t, A, diag1[:, t], 4 + t)
            pe.wait_ge(d_pw, 16)
            branches(0)
            branches(1)
            for f in range(3):
                for g in range(2):
                    if (f, g) in PE_HELPS:
                        taps(f, g)
                    fusion(f, g)
            for group, done in (((0, 1), 22), ((2, 3, 4), 24)):
                pe.wait_ge(pw_ev, done)
                if group[0] == 0:
                    pe.wait_ge(d_misc, 32)
                for t in group:
                    c = slice(t * P, min((t + 1) * P, NPX))
                    w = c.stop - c.start
                    nc.tensor.transpose(ps[0:w, t, 0:P], act_a[:, 0, c], id_s[:])
                    last = nc.tensor.transpose(ps[0:w, t, P:D], act_a[LO, 1, c], id_s[LO, 0:DB])
                last.then_inc(tok_mm, 1)
            for t in range(NT):
                pe.wait_ge(ht_rdy, 2 * t + 2)
                last = nc.tensor.transpose(psf[:, 6 * 512 + t * P:6 * 512 + (t + 1) * P], ht[:, t, 0:P], id_s[:])
            last.then_inc(xt_mm, 1)
            for t in range(NT):
                last = nc.tensor.transpose(psf[:, t * P:(t + 1) * P], ht[:, t, P:256], id_s[:])
            last.then_inc(xt_mm, 1)
            pe.wait_ge(xa_rdy, 1)
            pe.wait_ge(xf_rdy, 1)
            for t in range(NT):
                c = slice(t * P, (t + 1) * P)
                gw = V["gate_w"]
                mm(ps[:, 4, t * E:(t + 1) * E], xf[:, 0, c], vecs[:, gw:gw + E], start=True, stop=False)
                last = mm(ps[:, 4, t * E:(t + 1) * E], xf[LO, 1, c], vecs[LO, gw + E:gw + 2 * E],
                          start=False, stop=True)
            last.then_inc(lg_mm, 1)
            for h in range(2):
                c = slice(h * HT, (h + 1) * HT)
                mm(ps[0:64, 2 + h, 0:HT], vw64[:, 0, :], xf[:, 0, c], start=True, stop=False)
                last = mm(ps[0:64, 2 + h, 0:HT], vw64[LO, 1, :], xf[LO, 1, c], start=False, stop=True)
            last.then_inc(v_mm, 1)
            pe.sem_inc(l2_mm, RING)

            def first_product(slot, k, hs):
                f = slice(k * P, (k + 1) * P)
                for h in range(2):
                    c = slice(h * HT, (h + 1) * HT)
                    o = ps[:, 2 * hs + h, 0:HT]
                    mm(o, w1h[:, slot, 0, f], xh[:, c], start=True, stop=False)
                    mm(o, w1h[:, slot, 0, f], xl[:, c], start=False, stop=False)
                    mm(o, w1l[:, slot, 0, f], xh[:, c], start=False, stop=False)
                    mm(o, w1h[:, slot, 1, f], xb[:, c], start=False, stop=False)
                    last = mm(o, w1l[LO, slot, 1, f], xb[LO, c], start=False, stop=True)
                return last

            def second_product(slot, k, r):
                for h in range(2):
                    c = slice(h * HT, (h + 1) * HT)
                    oa, ob = ps[:, 4 + h, 0:HT], ps[:, 6 + h, 0:HT]
                    mm(oa, w2s[:, slot, k, 0:P], hh[:, r, c], start=False, stop=False)
                    mm(oa, w2s[:, slot, k, 256:384], hh[:, r, c], start=False, stop=False)
                    mm(ob, w2s[:, slot, k, P:256], hh[:, r, c], start=False, stop=False)
                    mm(oa, w2s[:, slot, k, 0:P], hl[:, r, c], start=False, stop=False)
                    last = mm(ps[LO, 6 + h, 0:HT], w2s[:, slot, k, P:D], hl[:, r, c], start=False, stop=False)
                return last

            pe.wait_ge(xs_rdy, 3)
            pe.wait_ge(lo1, 1)
            first_product(0, 0, 0).then_inc(l1_mm, 1)
            pe.wait_ge(v_ev, 1)
            first_product(0, 1, 1).then_inc(l1_mm, 1)
            pe.wait_ge(comb_rdy, 1)
            for t in range(NT):
                last = nc.tensor.transpose(psf[0:2 * E, 6 * 512 + t * P:6 * 512 + (t + 1) * P], comb2[:, t, :].bitcast(F32), id_s[:])
            last.then_inc(combt_mm, 1)
            pe.wait_ge(combt_rdy, 1)
            pe.wait_ge(zeroed, 4)
            for e in range(E):
                if e in (2, 4):
                    pe.wait_ge(h_read, e // 2 + 2)
                    first_product(0, e // 2 + 1, (e // 2 + 1) % 2).then_inc(l1_mm, 1)
                b = 4 + 2 * (e % 2)
                if e >= 2:
                    pe.wait_ge(cb_odd if e % 2 else cb_even, e // 2)
                for h in range(2):
                    last = mm(ps[:, b + h, 0:HT], selr[:, e * P:(e + 1) * P], combt[:, h * HT:(h + 1) * HT],
                              start=True, stop=True)
                last.then_inc(cb_mm, 1)
            pe.wait_ge(cb_even, E // 2)
            pe.wait_ge(cb_odd, E // 2)
            for b in range(4, 8):
                mm(ps[:, b, 0:HT], zeror[:], combt[:, 0:HT], start=True, stop=False)
            def pair_of_experts(i, last):
                for sl in range(2 * FK):
                    j, k = divmod(sl, FK)
                    s = i * 2 * FK + sl
                    if k == 0:
                        pe.wait_ge(lo2, i * 4 + 2 * (j + 1))
                    pe.wait_ge(hl_rdy, s + 2)
                    second_product(j, k, sl % RING).then_inc(l2_mm, 1)
                    if last and sl + LAG >= 2 * FK:
                        continue
                    j1, k1 = divmod(sl + LAG, FK)
                    if k1 == 0:
                        pe.wait_ge(lo1, i * 2 + (j1 + 1))
                    pe.wait_ge(h_read, s + (LAG + 1))
                    first_product(j1 % 2, k1, sl % 2).then_inc(l1_mm, 1)

            with pe.Fori(0, E // 2 - 1) as i:
                pair_of_experts(i, False)
            pair_of_experts(E // 2 - 1, True)
            pe.wait_ge(bk_rdy, 7)
            pe.wait_ge(ow_rdy, 2)
            for h in range(2):
                c = slice(h * HT, (h + 1) * HT)
                mm(ps[:, 4 + h, 0:HT], ow[:, 0:P], gm[:, c], start=False, stop=True)
                last = mm(ps[:, 6 + h, 0:HT], ow[:, P:2 * P], gm[:, c], start=False, stop=True)
            last.then_inc(y_mm, 1)
            for t in range(NT):
                if t in (0, 2):
                    pe.wait_ge(y_ev, 2 + t)
                c = slice(t * P, min((t + 1) * P, TOK))
                w = c.stop - c.start
                bank, off = (0, 2)[t // 2 % 2] + t // 4, (t % 2) * D
                nc.tensor.transpose(ps[0:w, bank, off:off + P], yt[:, 0, c], id_s[:])
                last = mm(ps[0:w, bank, off + P:off + D], yt[:, 1, c], pair_s[:], start=True, stop=True)
                if t % 2 or t == NT - 1:
                    last.then_inc(yt_mm, 1)


def haar_matrix():
    k = np.arange(256)[:, None]
    px = np.arange(256)[None, :]
    r, c = px // 16, px % 16
    s = np.zeros((256, 256), np.int64)
    for lv in range(4):
        band = (k >> (2 * (3 - lv))) & 3
        s += (band >> 1) * ((c >> lv) & 1) + (band & 1) * ((r >> lv) & 1)
    return np.where(s % 2, -0.0625, 0.0625).astype(np.float32)


def kernel(**inputs):
    import concourse.bacc as bacc
    from concourse.bass_utils import run_bass_kernel_spmd

    t = {k.replace("L0_tok_", "").replace("L0_attn_", "").replace("L0_ffn_", "f_"): np.asarray(v)
         for k, v in inputs.items()}
    f32 = np.float32

    def parts(v):
        v = v.reshape(D, -1)
        o = np.zeros((P, 2, v.shape[1]), f32)
        o[:, 0] = v[:P]
        o[:DB, 1] = v[P:]
        return o

    def three(a, g):
        a, g = a.reshape(D, -1), g.reshape(D, -1)
        return np.stack([a[:P], np.concatenate([a[P:], g[P:]]), g[:P]], 1)

    vec = np.zeros((P, NVEC), f32)

    def put(name, v):
        v = v.reshape(P, -1)
        vec[:, V[name]:V[name] + v.shape[1]] = v

    put("dw1", three(t["pl_dw"], t["pg_dw"]))
    put("dwf", np.stack([parts(t[f"f{i}_dw"]) for i in (1, 2, 3)], 1))
    put("bias1", three(t["pl_b"], t["pg_b1"]))
    put("bias2", three(t["pl_pwb"], t["pg_pwb"]))
    put("b_w2", parts(t["pg_b2"]))
    put("alpha", parts(t["alpha"]))
    put("fb", np.stack([parts(t[f"f{i}_pwb"]) for i in (1, 2, 3)], 1))
    put("v_w", parts(t["f_v_w"]))
    put("bk", parts(t["f_bk_scale"]))
    put("out_b", parts(t["f_out_b"]))
    put("gate_w", parts(t["f_gate_w"]))
    put("v_b", np.broadcast_to(t["f_v_b"].reshape(1, 1), (P, 1)))
    put("b1", t["f_b1"].reshape(E, FK, P).transpose(2, 0, 1))

    x = t["x"].reshape(2, HB, CIN, G, PATCH, G, PATCH).transpose(0, 2, 4, 6, 3, 5, 1)
    x = x.reshape(2, KT, P, HPX).transpose(0, 2, 1, 3)
    plw = t["pl_w"].reshape(D, KP).T.reshape(KT, P, D).transpose(1, 0, 2)
    w1t = t["pg_w1"].reshape(D, 256, CIN)
    w1t = np.concatenate([w1t[P:], w1t[:P]]).transpose(1, 2, 0).reshape(2, P, CIN * D).transpose(1, 0, 2)
    had = haar_matrix().reshape(2, P, 256).transpose(1, 0, 2)
    pw = np.zeros((P, 6, 2, D), f32)
    for i, (name, rows) in enumerate([("pl_pw", 0), ("pg_pw", DB), ("pg_w2", DB), ("f1_pw", 0), ("f2_pw", 0),
                                      ("f3_pw", 0)]):
        w = t[name].reshape(D, D).T
        pw[:, i, 0] = w[:P]
        pw[rows:rows + DB, i, 1] = w[P:]
    projw = np.zeros((P, 3 * D), f32)
    projw[:, :2 * D] = parts(t["proj_w"].T).reshape(P, 2 * D)
    projw[0, 2 * D:] = t["proj_b"]
    rows = np.concatenate([t["ln_g"], t["ln_b"], t["f_gate_b"], t["f_bk_scale"]]).reshape(1, -1)
    ident = np.eye(P, dtype=f32)
    pair = np.concatenate([np.eye(DB, dtype=f32)] * 2)
    sel = np.zeros((2, E, E, P), f32)
    for e in range(E):
        sel[:, e, e] = 1.0
    arrays = {
        "x": x, "vec": vec, "rows": rows, "had": had, "w1t": w1t, "plw": plw, "pw": pw, "projw": projw,
        "cls": t["cls"].reshape(1, D), "ident": ident, "pair": pair, "sel": sel.reshape(2 * E, E * P),
        "w1": t["f_w1"], "w2": t["f_w2"].reshape(E, FK, P, D).transpose(0, 2, 1, 3), "b2": t["f_b2"],
        "outw": t["f_out_w"],
    }
    nc = bacc.Bacc("TRN2", target_bir_lowering=False, num_devices=1)
    arrays = {k: np.ascontiguousarray(v) for k, v in arrays.items()}
    args = {k: nc.dram_tensor("in_" + k, v.shape, mybir.dt.from_np(v.dtype), kind="ExternalInput").ap()
            for k, v in arrays.items()}
    out = nc.dram_tensor("out_tokens", (TOK, D), F32, kind="ExternalOutput").ap()
    tower(nc, out=out, **args)
    r = run_bass_kernel_spmd(nc, [{"in_" + k: v for k, v in arrays.items()}], core_ids=[0])
    got = np.asarray(r.results[0]["out_tokens"])
    px = got[:NPX].reshape(2, G * G, HB, D).transpose(0, 2, 1, 3).reshape(B, G * G, D)
    return np.concatenate([got[NPX:][:, None], px], axis=1)
```

```python
from contextlib import ExitStack

import numpy as np

import concourse.bass as bass
from concourse import mybir

F32 = mybir.dt.float32
F32R = mybir.dt.float32r
ALU = mybir.AluOpType
ACT = mybir.ActivationFunctionType
AX = mybir.AxisListType

P = 128
B, CIN, PATCH, G = 16, 3, 16, 6
NPX = G * G * B
HPX = NPX // 2
HB = B // 2
D = 192
DB = D - P
KP = CIN * PATCH * PATCH
KT = KP // P
TOK = NPX + B
NT = -(-TOK // P)
LAST = NPX - (NT - 1) * P
SEQ = G * G + 1
E, F = 8, 768
FT = NPX + 4
FH = FT // 2
FK = F // P
EPS = 1e-5
LAG = 4
RING = 4
K_HI2, K_HI1 = 2, 4
PE_TAPS = [(-1, 0), (-1, -1), (-1, 1)]
PE_HELPS = [(0, 1), (1, 0), (1, 1), (2, 0), (2, 1)]
TAPS = [(0, 0)] + [(dy, dx) for dy in (-1, 0, 1) for dx in (-1, 0, 1) if (dy, dx) != (0, 0)]

V = {}
_n = 0
for _name, _w in [("dw1", 27), ("dwf", 54), ("bias1", 3), ("bias2", 3), ("b_w2", 2), ("alpha", 2), ("fb", 6),
                  ("bk", 2), ("out_b", 2), ("gate_w", 2 * (E + 1)), ("v_b", 1), ("b1", E * FK)]:
    V[_name] = _n
    _n += _w
NVEC = _n


def tower(nc, x, vec, rows, had, w1t, plw, pw, projw, cls, ident, layout, sel, w1, w2, b2, outw, out):
    with ExitStack() as ctx:
        def sb(name, shape, dt=F32):
            return ctx.enter_context(nc.sbuf_tensor(name, shape, dt))

        def sem(name):
            return ctx.enter_context(nc.semaphore(name))

        ps = ctx.enter_context(nc.psum_tensor("ps", [P, 8, 512], F32))
        psf = ps[:].rearrange("p k n -> p (k n)")

        vecs = sb("vecs", [P, NVEC])
        rowb = sb("rowb", [P, 2 * D + E])
        had_s = sb("had_s", [P, 2, 256])
        w1t_s = sb("w1t_s", [P, 2, CIN * D])
        x_s = sb("x_s", [P, KT, NPX])
        embed = sb("embed", [P, KT, 2 * D])
        pw_s = sb("pw_s", [P, 6, 2, D])
        proj_s = sb("proj_s", [P, 2, D])
        projb_s = sb("projb_s", [1, D])
        id_s = sb("id_s", [P, P])
        layout_s = sb("layout_s", [P, DB + P // HB + 2 * DB])
        pair_s = layout_s[:, 0:DB]
        blk_s = layout_s[:, DB:DB + P // HB]
        img_s = layout_s[:, DB + P // HB:].rearrange("p (g m) -> p g m", g=2)
        sel_s = sb("sel_s", [2 * E, E * P])
        cls_s = sb("cls_s", [P, D])
        conv = sb("conv", [P, 3, 3, NPX])
        act_a, act_b = conv[:, 0], conv[:, 1]
        loc = conv[:, 2]
        glob = sb("glob", [P, 2, NPX])
        gate = sb("gate", [P, 8])
        zt = sb("zt", [P, NT, D])
        ht = sb("ht", [P, NT, D])
        stats = sb("stats", [P, NT, 6])
        mv = sb("mv", [P, NT, 2])
        var = sb("var", [P, NT])
        rstd = sb("rstd", [P, NT])
        neghalf = sb("neghalf", [P, NT + 1])
        zero = sb("zero", [P, P])
        ones = sb("ones", [1, P])
        zeror = sb("zeror", [2 * E, P], F32R)
        attn = sb("attn", [P, D])
        xf = sb("xf", [P, 2, NT * P])
        xh = sb("xh", [P, FT], F32R)
        xl = sb("xl", [P, FT], F32R)
        xb = sb("xb", [P, FT], F32R)
        lg = sb("lg", [P, NT, E])
        lgt = sb("lgt", [P, NT, E, E])
        lge = sb("lge", [P, NT, E, E])
        rk = sb("rk", [P, NT, E])
        sc = sb("sc", [P, 4, NT])
        comb = sb("comb", [P, NT, E])
        comb2 = sb("comb2", [P, NT, 2 * E], F32R)
        combt = sb("combt", [2 * E, NT * P], F32R)
        selr = sb("selr", [2 * E, E * P], F32R)
        cb = conv[:].rearrange("p a t c -> p (a t c)")[:, 0:E * FT].rearrange("p (e c) -> p e c", e=E)
        vt = sb("vt", [P, NT, P // HB])
        w1raw = sb("w1raw", [P, 2, 2, F])
        w2raw = sb("w2raw", [P, 2, FK, D])
        w1h = sb("w1h", [P, 2, 2, F], F32R)
        w1l = sb("w1l", [P, 2, 2, F], F32R)
        w2s = sb("w2s", [P, 2, FK, 2 * D], F32R)
        hgw = sb("hgw", [P, 4, FT])
        hg, hw = hgw[:, 0:2], hgw[:, 2:4]
        diag = hgw[:].rearrange("p a c -> p (a c)")[:, 0:18 * P].rearrange("p (f t m k) -> p f t m k", f=3, t=2, m=3)
        hh = sb("hh", [P, RING, FT], F32R)
        hl = sb("hl", [P, RING, FT], F32R)
        xbh = hh[:, RING - 1]
        yt = x_s[:].rearrange("p k c -> p (k c)")[:, 0:2 * TOK].rearrange("p (t c) -> p t c", t=2)
        ycls = sb("ycls", [P, 2])
        vseq = sb("vseq", [64, SEQ])
        ar = sb("ar", [64, SEQ, 2])
        tr = sb("tr", [64, SEQ + 2, 2])
        sw = sb("sw", [64, 2, 2])
        phi = sb("phi", [B, SEQ, 2])
        zz = sb("zz", [B, 6, SEQ])
        wi = sb("wi", [B, 8])
        ft = sb("ft", [B, 2, SEQ])
        gm = x_s[:].rearrange("p k c -> p (k c)")[0:80, 2 * TOK:2 * TOK + FT + B]
        ow = sb("ow", [80, 2 * P])
        bkr = sb("bkr", [48, D])

        d_id = sem("ld_id")
        d_had, d_vec, d_plw, d_pw, d_misc, d_proj, d_ffn, d_cls, d_rows = [
            sem("ld_" + n) for n in ("had", "vec", "plw", "pw", "misc", "proj", "ffn", "cls", "rows")]
        d_x = [sem(f"ld_x{k}") for k in range(4)]
        d_w = [sem("ld_w0"), sem("ld_w1")]
        d_out = sem("stored")
        diag_rdy = sem("diag_rdy")
        mid_tap = sem("mid_tap")
        tap_mm = sem("tap_mm")
        had_mm = sem("had_mm")
        had_cp = sem("had_cp")
        emb_mm = sem("emb_mm")
        gelu1 = sem("gelu1")
        dw_done = sem("dw_done")
        pw_mm = sem("pw_mm")
        pw_ev = sem("pw_ev")
        gates = sem("gates")
        mixed = sem("mixed")
        vt_rdy = sem("vt_rdy")
        v_done = sem("v_done")
        a_done = sem("a_done")
        p_done = sem("p_done")
        zeroed = sem("zeroed")
        attn_mm = sem("attn_mm")
        attn_rdy = sem("attn_rdy")
        tok_mm = sem("tok_mm")
        var_rdy = sem("var_rdy")
        rstd_rdy = sem("rstd_rdy")
        ht_rdy = sem("ht_rdy")
        xt_mm = sem("xt_mm")
        xf_rdy = sem("xf_rdy")
        xa_rdy = sem("xa_rdy")
        xs_rdy = sem("xs_rdy")
        lg_mm = sem("lg_mm")
        lg_max = sem("lg_max")
        lg_exp = sem("lg_exp")
        comb_rdy = sem("comb_rdy")
        combt_mm = sem("combt_mm")
        combt_rdy = sem("combt_rdy")
        v_mm = sem("v_mm")
        v_ev = sem("v_ev")
        vseq_rdy = sem("vseq_rdy")
        cb_mm = sem("cb_mm")
        cb_even = sem("cb_even")
        cb_odd = sem("cb_odd")
        hi1 = sem("hi1")
        hi2 = sem("hi2")
        lo1 = sem("lo1")
        lo2 = sem("lo2")
        l1_mm = sem("l1_mm")
        h_read = sem("h_read")
        hw_rdy = sem("hw_rdy")
        hh_rdy = sem("hh_rdy")
        hl_rdy = sem("hl_rdy")
        l2_mm = sem("l2_mm")
        bk_rdy = sem("bk_rdy")
        ow_zero = sem("ow_zero")
        ow_rdy = sem("ow_rdy")
        y_mm = sem("y_mm")
        y_ev = sem("y_ev")
        y_evb = sem("y_evb")
        yt_mm = sem("yt_mm")
        fin_rdy = sem("fin_rdy")

        def vcol(name, i=0, rows=slice(0, P)):
            return vecs[rows, V[name] + i:V[name] + i + 1]

        A, LO, HI = slice(0, P), slice(0, DB), slice(DB, P)
        groups = ((0, 1), tuple(range(2, NT)))
        tok_ps = [ps[:, b, o:o + D] for b, o in ((0, 0), (0, D), (1, 0), (1, D), (2, 0))]
        xa_ps, xb_ps, xc_ps = (ps[:, 4], ps[:, 3]), (ps[:, 5], ps[:, 6]), (ps[:, 7], ps[:, 0])
        lg_ps = ps[:, 4, 256:256 + NT * (E + 1)].rearrange("p (t e) -> p t e", t=NT)
        v_ps = ps[0:DB, 7, 320:320 + SEQ]
        combt_ps = psf[0:2 * E, 5 * 512:5 * 512 + NT * P]

        def group_cols(g, end):
            lo = P * groups[g][0]
            hi = min(P * (groups[g][-1] + 1), end)
            return slice(lo, hi), slice(0, hi - lo)

        block = ctx.enter_context(nc.Block())

        def load_expert(q, e, slot):
            q.dma_start(w1raw[:, slot, 0, :], w1[e, 0:P, :]).then_inc(d_w[slot], 16)
            q.dma_start(w1raw[LO, slot, 1, :], w1[e, P:D, :]).then_inc(d_w[slot], 16)
            q.dma_start(w1raw[HI, slot, 1, :], w1[e, P:D, :]).then_inc(d_w[slot], 16)
            q.dma_start(w2raw[:, slot, :, :], w2[e]).then_inc(d_w[slot], 16)

        @block.sync
        def _(sp):
            sp.dma_start(had_s[:], had).then_inc(d_had, 16)
            sp.dma_start(embed[:, :, 0:D], plw).then_inc(d_plw, 16)
            for g in range(2):
                for kh in range(2):
                    ks = slice(kh * KT // 2, (kh + 1) * KT // 2)
                    sp.dma_start(x_s[:, ks, g * HPX:(g + 1) * HPX], x[g, :, ks, :]).then_inc(d_x[2 * g + kh], 16)
            sp.dma_start(pw_s[:], pw).then_inc(d_pw, 16)
            sp.dma_start(layout_s[:], layout).then_inc(d_misc, 16)
            sp.dma_start(sel_s[:], sel).then_inc(d_misc, 16)
            load_expert(sp, 0, 0)
            load_expert(sp, 1, 1)
            for e in range(2, E):
                sp.wait_ge(lo1, e - 1)
                sp.wait_ge(lo2, 2 * (e - 1))
                load_expert(sp, e, e % 2)
            for t in (0, 2, NT - 1):
                sp.wait_ge(fin_rdy, t + 1)
                w = min(P, TOK - P * t)
                sp.dma_start(out[t * P:t * P + w, :], zt[0:w, t, :]).then_inc(d_out, 16)
            sp.wait_ge(d_out, 16 * NT)

        def spectral(pool):
            n = 4
            pool.wait_ge(vseq_rdy, 2)
            nc.gpsimd.memset(gm, 0.0).then_inc(p_done, 1)
            n += 1
            pool.wait_ge(p_done, n)
            for i in range(SEQ):
                nc.gpsimd.tensor_tensor(sw[:, 0, :], tr[:, i, :], tr[:, i + 1, :], ALU.add).then_inc(p_done, 1)
                nc.gpsimd.tensor_tensor(sw[:, 1, :], ar[:, i, :], tr[:, i + 1, ::-1], ALU.mult).then_inc(p_done, 1)
                n += 2
                pool.wait_ge(p_done, n)
                nc.gpsimd.tensor_tensor(tr[:, i + 2, :], sw[:, 0, :], sw[:, 1, :], ALU.add).then_inc(p_done, 1)
                n += 1
                pool.wait_ge(p_done, n)

            def link(ins):
                nonlocal n
                ins.then_inc(p_done, 1)
                n += 1
                pool.wait_ge(p_done, n)

            link(nc.gpsimd.tensor_scalar(wi[:, 0:2], tr[0:B, SEQ + 1, :], 2.0 ** -60, None, ALU.mult))
            link(nc.gpsimd.tensor_tensor(wi[:, 2:4], wi[:, 0:2], wi[:, 0:2], ALU.mult))
            link(nc.gpsimd.tensor_tensor(wi[:, 4:5], wi[:, 2:3], wi[:, 3:4], ALU.add))
            link(nc.gpsimd.tensor_tensor(wi[:, 5:6], wi[:, 4:5], neghalf[0:B, NT:NT + 1], ALU.pow))
            link(nc.gpsimd.tensor_copy(phi[:], tr[32:32 + B, SEQ:0:-1, :]))
            th = tr[0:B, 1:SEQ + 1, :]
            link(nc.gpsimd.tensor_tensor(zz[:, 0, :], th[:, :, 0], phi[:, :, 0], ALU.mult))
            link(nc.gpsimd.tensor_tensor(zz[:, 1, :], th[:, :, 1], phi[:, :, 1], ALU.mult))
            link(nc.gpsimd.tensor_tensor(zz[:, 2, :], th[:, :, 0], phi[:, :, 1], ALU.mult))
            link(nc.gpsimd.tensor_tensor(zz[:, 3, :], th[:, :, 1], phi[:, :, 0], ALU.mult))
            link(nc.gpsimd.tensor_tensor(zz[:, 0, :], zz[:, 0, :], zz[:, 1, :], ALU.subtract))
            link(nc.gpsimd.tensor_tensor(zz[:, 1, :], zz[:, 2, :], zz[:, 3, :], ALU.add))
            link(nc.gpsimd.tensor_scalar(wi[:, 6:8], wi[:, 0:2], wi[:, 5:6], 2.0 ** -60, ALU.mult, ALU.mult))
            link(nc.gpsimd.tensor_scalar(zz[:, 2, :], zz[:, 0, :], wi[:, 6:7], None, ALU.mult))
            link(nc.gpsimd.tensor_scalar(zz[:, 3, :], zz[:, 1, :], wi[:, 7:8], None, ALU.mult))
            link(nc.gpsimd.tensor_scalar(zz[:, 4, :], zz[:, 1, :], wi[:, 6:7], None, ALU.mult))
            link(nc.gpsimd.tensor_scalar(zz[:, 5, :], zz[:, 0, :], wi[:, 7:8], None, ALU.mult))
            link(nc.gpsimd.tensor_tensor(ft[:, 0, :], zz[:, 5, :], zz[:, 4, :], ALU.subtract))
            link(nc.gpsimd.tensor_tensor(ft[:, 1, :], zz[:, 2, :], zz[:, 3, :], ALU.add))
            pool.wait_ge(combt_rdy, 1)
            nc.gpsimd.tensor_copy(gm[64:64 + 2 * E, 0:NPX], combt[:, 0:NPX].bitcast(F32)).then_inc(bk_rdy, 1)
            nc.gpsimd.tensor_copy(gm[64:64 + 2 * E, FT:], combt[:, NPX:TOK].bitcast(F32)).then_inc(bk_rdy, 1)
            link(nc.gpsimd.tensor_scalar(ft[:], ft[:], 10.0, -10.0, ALU.min, ALU.max))
            for f in range(2):
                r = slice(32 * f, 32 * f + B)
                mask = id_s[0:B, 0:B]
                for g in range(2):
                    nc.gpsimd.tensor_tensor(
                        gm[r, g * HPX:(g + 1) * HPX].rearrange("p (n b) -> p n b", b=HB),
                        ft[:, f, 1:SEQ].unsqueeze(2).to_broadcast([B, SEQ - 1, HB]),
                        mask[:, g * HB:(g + 1) * HB].unsqueeze(1).to_broadcast([B, SEQ - 1, HB]),
                        ALU.mult).then_inc(bk_rdy, 1)
                nc.gpsimd.tensor_tensor(gm[r, FT:], ft[:, f, 0:1].to_broadcast([B, B]), mask,
                                        ALU.mult).then_inc(bk_rdy, 1)

        @block.gpsimd
        def _(pool):
            nc.gpsimd.memset(neghalf[:, 0:NT], -0.5).then_inc(p_done, 1)
            nc.gpsimd.memset(neghalf[:, NT:], -1.0).then_inc(p_done, 1)
            nc.gpsimd.memset(tr[:], 0.0).then_inc(p_done, 1)
            nc.gpsimd.memset(ow[:], 0.0).then_inc(ow_zero, 1)
            pool.wait_ge(p_done, 3)
            nc.gpsimd.memset(tr[:, 1:2, 0:1], 1.0).then_inc(p_done, 1)
            pool.wait_ge(d_vec, 16)
            pool.wait_ge(d_id, 16)
            for f in range(3):
                for t in range(2):
                    for m, (dy, dx) in enumerate(PE_TAPS):
                        tap = V["dwf"] + 18 * f + 9 * t + (dy + 1) * 3 + dx + 1
                        nc.gpsimd.tensor_scalar(diag[:, f, t, m, :], id_s[:], vecs[:, tap:tap + 1], None,
                                                ALU.mult).then_inc(diag_rdy, 1)
            for k, grp in enumerate((0, 0, 1, 1, 0, 1)):
                ts = (slice(0, 2), slice(2, NT))[grp]
                pool.wait_ge(var_rdy, k + 1)
                nc.gpsimd.tensor_tensor(rstd[:, ts], var[:, ts], neghalf[:, ts], ALU.pow).then_inc(rstd_rdy, 1)
                if k == 3:
                    spectral(pool)

        @block.scalar
        def _(act):
            act.dma_start(w1t_s[:], w1t).then_inc(d_had, 16)
            act.dma_start(vecs[:], vec).then_inc(d_vec, 16)
            act.dma_start(id_s[:], ident).then_inc(d_id, 16)
            act.dma_start(proj_s[:], projw[:, 0:2 * D].rearrange("p (t d) -> p t d", t=2)).then_inc(d_proj, 16)
            act.dma_start(projb_s[:], projw[0:1, 2 * D:3 * D]).then_inc(d_proj, 16)
            act.dma_start(cls_s[LAST:LAST + B, :], cls.to_broadcast([B, D])).then_inc(d_cls, 16)
            act.dma_start(rowb[:], rows[0:1, 0:2 * D + E].to_broadcast([P, 2 * D + E])).then_inc(d_rows, 16)
            act.wait_ge(ow_zero, 1)
            for f in range(2):
                act.dma_start(ow[32 * f:32 * f + B, 0:D], outw[f:f + 1, :].to_broadcast([B, D])).then_inc(d_ffn, 16)
                act.dma_start(bkr[32 * f:32 * f + B, :],
                              rows[0:1, 2 * D + E:3 * D + E].to_broadcast([B, D])).then_inc(d_ffn, 16)
                act.dma_start(ow[64 + E * f:64 + E * f + E, 0:D], b2).then_inc(d_ffn, 16)
            act.wait_ge(d_vec, 16)
            nc.scalar.activation(gate[:, 0:2], vecs[:, V["alpha"]:V["alpha"] + 2], ACT.Tanh).then_inc(a_done, 1)
            for pt in range(2):
                act.wait_ge(had_mm, pt + 1)
                b = 4 + 2 * pt
                nc.scalar.copy(embed[:, pt:pt + 3:2, D:2 * D],
                               ps[:, b, 0:2 * D].rearrange("p (c n) -> p c n", c=2)).then_inc(had_cp, 1)
                nc.scalar.copy(embed[:, 4 + pt, D:2 * D], ps[:, b + 1, 0:D]).then_inc(had_cp, 1)

            def px(g):
                return slice(g * HPX, (g + 1) * HPX)

            def embed_out(g):
                for t in range(3):
                    act.wait_ge(emb_mm, 3 * g + t + 1)
                    nc.scalar.activation(act_a[:, t, px(g)], ps[:, 4 * g + t, 0:HPX], ACT.Gelu,
                                         bias=vcol("bias1", t)).then_inc(gelu1, 1)
                    act.wait_ge(gelu1, 3 * g + t + 1)
                    middle_tap(g, t, A, V["dw1"])

            def middle_tap(g, t, rows_, taps):
                nc.scalar.activation(act_b[rows_, t, px(g)], act_a[rows_, t, px(g)], ACT.Identity,
                                     scale=vecs[rows_, taps + 9 * t + 4:taps + 9 * t + 5]).then_inc(mid_tap, 1)

            def evacuate(n, bank, dst, rows_, func, bias, scale=1.0):
                act.wait_ge(pw_mm, n)
                nc.scalar.activation(dst, ps[rows_, bank, 0:HPX], func, bias=bias, scale=scale).then_inc(pw_ev, 1)

            def branches(g):
                b, n = 4 * g, 6 * g
                evacuate(n + 1, b + 2, loc[:, 2, px(g)], A, ACT.Gelu, vcol("bias2", 2))
                evacuate(n + 2, b + 1, loc[HI, 1, px(g)], HI, ACT.Gelu, vcol("bias2", 1, HI))
                evacuate(n + 3, b, loc[:, 0, px(g)], A, ACT.Identity, vcol("bias2", 0))
                evacuate(n + 4, b + 1, loc[LO, 1, px(g)], LO, ACT.Identity, vcol("bias2", 1, LO))
                if g == 0:
                    act.wait_ge(gates, 1)
                evacuate(n + 5, b + 2, glob[:, 0, px(g)], A, ACT.Identity, gate[:, 6:7], gate[:, 2:3])
                evacuate(n + 6, b + 3, glob[LO, 1, px(g)], LO, ACT.Identity, gate[LO, 7:8], gate[LO, 3:4])

            def fusion(f, g):
                n, b = 12 + 4 * f + 2 * g, 4 * g
                fn = ACT.Relu if f < 2 else ACT.Identity
                evacuate(n + 1, b, act_a[:, 0, px(g)], A, fn, vcol("fb", 2 * f))
                evacuate(n + 2, b + 1, act_a[LO, 1, px(g)], LO, fn, vcol("fb", 2 * f + 1, LO))
                if f == 0:
                    act.wait_ge(pw_ev, n + 2)
                    for t, rows_ in ((0, A), (1, LO)):
                        middle_tap(g, t, rows_, V["dwf"] + 18)

            def split_hi1(slot):
                nc.scalar.copy(w1h[:, slot, :, :], w1raw[:, slot, :, :]).then_inc(hi1, 1)

            def split_hi2(slot):
                nc.scalar.copy(w2s[:, slot, :, 0:D], w2raw[:, slot, :, :]).then_inc(hi2, 1)

            embed_out(0)
            embed_out(1)
            act.wait_ge(attn_mm, 1)
            nc.scalar.copy(attn[:], ps[:, 3, 0:D]).then_inc(attn_rdy, 1)
            branches(0)
            branches(1)
            for f in range(3):
                for g in range(2):
                    fusion(f, g)
                    if (f, g) == (1, 0):
                        act.wait_ge(d_w[0], 64)
                        split_hi1(0)
                        split_hi2(0)

            act.wait_ge(d_w[1], 64)
            split_hi1(1)
            for g in range(2):
                (c, cp), (ct, _) = group_cols(g, NT * P), group_cols(g, FT)
                act.wait_ge(xt_mm, 3 * g + 1)
                nc.scalar.copy(xf[:, 0, c], xa_ps[g][:, cp]).then_inc(xa_rdy, 1)
                act.wait_ge(xt_mm, 3 * g + 2)
                nc.scalar.copy(xf[LO, 1, c], xb_ps[g][LO, cp]).then_inc(xf_rdy, 1)
                act.wait_ge(xa_rdy, 2 * g + 1)
                nc.scalar.copy(xh[:, ct], xf[:, 0, ct]).then_inc(xa_rdy, 1)
                act.wait_ge(xf_rdy, g + 1)
                nc.scalar.copy(xb[LO, ct], xf[LO, 1, ct]).then_inc(xs_rdy, 1)
            nc.scalar.sem_inc(h_read, 2)
            act.wait_ge(lg_max, 1)
            nc.scalar.activation(comb[:], lg[:], ACT.Exp).then_inc(lg_exp, 1)

            def gelu(i, sl):
                act.wait_ge(l1_mm, i * 2 * FK + (sl + 1))
                nc.scalar.activation(hg[:, sl % 2, :].rearrange("p (h n) -> p h n", h=2),
                                     ps[:, 2 * (sl % 2):2 * (sl % 2) + 2, 0:FH], ACT.Gelu_apprx_tanh,
                                     bias=vecs[:, bass.ds(i * 2 * FK + (V["b1"] + sl), 1)]).then_inc(h_read, 1)

            def pair_of_experts(i, last):
                for sl in range(2 * FK):
                    j, k = divmod(sl, FK)
                    s = i * 2 * FK + sl
                    act.wait_ge(hw_rdy, s + 1)
                    act.wait_ge(l2_mm, s + 1)
                    nc.scalar.copy(hh[:, sl % RING, :], hw[:, sl % 2, :]).then_inc(hh_rdy, 1)
                    if not (last and sl >= 2 * FK - 2):
                        gelu(i, sl + 2)
                    if k == K_HI2 and not (last and j == 1):
                        act.wait_ge(l2_mm, i * 2 * FK + (j * FK + RING))
                        split_hi2(1 - j)
                    if k == K_HI1 and not last:
                        act.wait_ge(d_w[j], (i + 2) * 64)
                        split_hi1(j)

            gelu(0, 0)
            gelu(0, 1)
            for e in range(0, E, 2):
                for h in range(2):
                    act.wait_ge(cb_mm, 2 * e + h + 1)
                    nc.scalar.copy(cb[:, e, h * FH:(h + 1) * FH], ps[:, 4 + h, 0:FH]).then_inc(cb_even, 1)
            with act.Fori(0, E // 2 - 1) as i:
                pair_of_experts(i, False)
            pair_of_experts(E // 2 - 1, True)
            for h in range(2):
                act.wait_ge(y_mm, h + 1)
                c = slice(h * FH, min((h + 1) * FH, NPX))
                nc.scalar.activation(yt[:, 0, c], ps[:, 4 + h, 0:c.stop - c.start], ACT.Identity,
                                     bias=gate[:, 4:5]).then_inc(y_ev, 1)
            nc.scalar.activation(ycls[:, 0:1], ps[:, 5, NPX - FH:NPX - FH + 1], ACT.Identity,
                                 bias=gate[:, 4:5]).then_inc(y_ev, 1)
            act.wait_ge(y_ev, 3)
            nc.scalar.activation(yt[:, 0, NPX:TOK], ps[:, 5, FH:FH + B], ACT.Identity, bias=ycls[:, 0:1]).then_inc(y_ev, 1)
            for t in (1, 3):
                act.wait_ge(fin_rdy, t + 1)
                act.dma_start(out[t * P:(t + 1) * P, :], zt[:, t, :]).then_inc(d_out, 16)

        @block.vector
        def _(dve):
            n = 0

            def own(ins):
                nonlocal n
                n += 1
                ins.then_inc(v_done, 1)
                return n

            def link(ins):
                dve.wait_ge(v_done, own(ins))

            nc.vector.memset(zero[:], 0.0).then_inc(zeroed, 1)
            nc.vector.memset(ones[:], 1.0).then_inc(zeroed, 1)
            nc.vector.memset(zeror[:].bitcast(F32), 0.0).then_inc(zeroed, 1)
            link(nc.vector.memset(zt[HI, NT - 1, :], 0.0))
            link(nc.vector.memset(mv[:], 0.0))
            dve.wait_ge(d_vec, 16)
            link(nc.vector.tensor_tensor(gate[:, 4:6], vecs[:, V["bk"]:V["bk"] + 2], vecs[:, V["out_b"]:V["out_b"] + 2],
                                         ALU.mult))
            dve.wait_ge(a_done, 1)
            link(nc.vector.tensor_scalar(gate[:, 2:4], gate[:, 0:2], 1.0, 0.5, ALU.add, ALU.mult))
            link(nc.vector.tensor_scalar(gate[:, 0:2], gate[:, 2:4], -1.0, 1.0, ALU.mult, ALU.add))
            nc.vector.tensor_tensor(gate[:, 6:8], gate[:, 2:4], vecs[:, V["b_w2"]:V["b_w2"] + 2],
                                    ALU.mult).then_inc(gates, 1)

            def depthwise(src, dst, taps, tiles, help_at=None, mid=None):
                mark = {}

                def rect(buf, g, t, rows_, dy, dx, sy, sx):
                    y0, y1, x0, x1 = max(0, -dy), G - max(0, dy), max(0, -dx), G - max(0, dx)
                    v = buf[rows_, t, g * HPX:(g + 1) * HPX].rearrange("p (y x) -> p y x", y=G)
                    return v[:, y0 + sy:y1 + sy, (x0 + sx) * HB:(x1 + sx) * HB]

                mine = [tp for tp in TAPS if (help_at is None or tp not in PE_TAPS) and (mid is None or tp != (0, 0))]
                for m, (dy, dx) in enumerate(mine):
                    tap = (dy + 1) * 3 + dx + 1
                    for k, (g, t, rows_) in enumerate(tiles):
                        o, a = rect(dst, g, t, rows_, dy, dx, 0, 0), rect(src, g, t, rows_, dy, dx, dy, dx)
                        w = vecs[rows_, taps + 9 * t + tap:taps + 9 * t + tap + 1]
                        if m == 0 and mid is None:
                            ins = nc.vector.tensor_scalar(o, a, w, None, ALU.mult)
                        else:
                            if m == 0:
                                dve.wait_ge(mid_tap, mid + k + 1)
                            else:
                                dve.wait_ge(v_done, mark[k])
                            ins = nc.vector.scalar_tensor_tensor(out=o, in0=a, scalar=w, in1=o, op0=ALU.mult,
                                                                 op1=ALU.add)
                        if help_at is None and m == len(mine) - 1:
                            ins.then_inc(dw_done, 1)
                        else:
                            mark[k] = own(ins)
                if help_at is not None:
                    for k, (g, t, rows_) in enumerate(tiles):
                        dve.wait_ge(tap_mm, help_at + k + 1)
                        dve.wait_ge(v_done, mark[k])
                        c = slice(g * HPX + G * HB, (g + 1) * HPX)
                        nc.vector.tensor_tensor(dst[rows_, t, c], ps[rows_, 4 * g + 2 + t, G * HB:HPX],
                                                dst[rows_, t, c], ALU.add).then_inc(dw_done, 1)

            def split_lo1(slot):
                nc.vector.tensor_tensor(w1l[:, slot, :, :], w1raw[:, slot, :, :],
                                        w1h[:, slot, :, :].bitcast(F32), ALU.subtract).then_inc(lo1, 1)

            def split_lo2(slot, part):
                a, o = ((slice(P, D), slice(D, 256)), (slice(0, P), slice(256, 2 * D)))[part]
                nc.vector.tensor_tensor(w2s[:, slot, :, o], w2raw[:, slot, :, a],
                                        w2s[:, slot, :, a].bitcast(F32), ALU.subtract).then_inc(lo2, 1)

            two = [(0, A), (1, LO)]
            at = 0
            for tiles in ([(0, 0, A)], [(0, 1, A)], [(0, 2, A), (1, 0, A)], [(1, 1, A), (1, 2, A)]):
                depthwise(act_a, act_b, V["dw1"], tiles, mid=at)
                at += len(tiles)
            for f in range(3):
                for g in range(2):
                    c = slice(g * HPX, (g + 1) * HPX)
                    if f == 0:
                        dve.wait_ge(pw_ev, 6 * g + 6)
                        for t, rows_ in two:
                            nc.vector.scalar_tensor_tensor(out=act_a[rows_, t, c], in0=loc[rows_, t, c],
                                                           scalar=gate[rows_, t:t + 1], in1=glob[rows_, t, c],
                                                           op0=ALU.mult, op1=ALU.add).then_inc(mixed, 1)
                        dve.wait_ge(mixed, 2 * g + 2)
                    else:
                        dve.wait_ge(pw_ev, 12 + 4 * (f - 1) + 2 * g + 2)
                    if f == 2:
                        for t, rows_ in two:
                            nc.vector.tensor_tensor(glob[rows_, t, c], act_a[rows_, t, c], loc[rows_, t, c],
                                                    ALU.add).then_inc(mixed, 1)
                        dve.wait_ge(mixed, 4 + 2 * g + 2)
                    src, dst = (act_a, act_a, glob)[f], act_b
                    depthwise(src, dst, V["dwf"] + 18 * f, [(g, t, r) for t, r in two],
                              2 * PE_HELPS.index((f, g)) if (f, g) in PE_HELPS else None,
                              6 + 2 * g if f == 1 else None)
            dve.wait_ge(hi1, 1)
            split_lo1(0)
            dve.wait_ge(hi2, 1)
            split_lo2(0, 0)
            split_lo2(0, 1)

            def norm_stats(src, tiles):
                for t, rows_ in tiles:
                    own(nc.vector.bn_stats(stats[rows_, t, :], src(t, rows_)))
                dve.wait_ge(v_done, n)
                for t, rows_ in tiles:
                    own(nc.vector.bn_aggr(mv[rows_, t, :], stats[rows_, t, :]))
                dve.wait_ge(v_done, n)
                ts = slice(tiles[0][0], tiles[-1][0] + 1)
                nc.vector.tensor_scalar(var[:, ts], mv[:, ts, 1], EPS, None, ALU.add).then_inc(var_rdy, 1)

            full = [(t, A) for t in range(NT)]
            cr = slice(LAST, LAST + B)
            last_px = [(NT - 1, slice(0, LAST))]
            dve.wait_ge(d_rows, 16)
            dve.wait_ge(attn_rdy, 1)
            dve.wait_ge(d_cls, 16)
            own(nc.vector.tensor_tensor(rowb[:, D:2 * D], rowb[:, D:2 * D], attn[:], ALU.add))
            own(nc.vector.tensor_tensor(zt[cr, NT - 1, :], cls_s[cr, :], attn[cr, :], ALU.add))

            tiles_of = (full[:2], full[2:-1] + last_px)

            def first_half(g):
                norm_stats(lambda t, r: tok_ps[t][r], tiles_of[g])
                for t, r in tiles_of[g]:
                    own(nc.vector.scalar_tensor_tensor(out=zt[r, t, :], in0=tok_ps[t][r], scalar=mv[r, t, 0:1],
                                                       in1=rowb[r, 0:D], op0=ALU.subtract, op1=ALU.mult))

            def first_scale(g, k):
                dve.wait_ge(v_done, n)
                dve.wait_ge(rstd_rdy, k)
                for t, r in tiles_of[g]:
                    own(nc.vector.scalar_tensor_tensor(out=zt[r, t, :], in0=zt[r, t, :], scalar=rstd[r, t:t + 1],
                                                       in1=rowb[r, D:2 * D], op0=ALU.mult, op1=ALU.add))
                dve.wait_ge(v_done, n)

            def second_scale(g, k):
                dve.wait_ge(rstd_rdy, k)
                for t in groups[g]:
                    nc.vector.tensor_scalar(ht[:, t, :], zt[:, t, :], mv[:, t, 0:1], rstd[:, t:t + 1],
                                            ALU.subtract, ALU.mult).then_inc(ht_rdy, 1)

            def split_tokens(g):
                ct, cp = group_cols(g, FT)
                dve.wait_ge(xt_mm, 3 * g + 3)
                link(nc.vector.tensor_copy(xbh[HI, ct], xc_ps[g][HI, cp]))
                nc.vector.tensor_tensor(xb[HI, ct], xc_ps[g][HI, cp], xbh[HI, ct].bitcast(F32),
                                        ALU.subtract).then_inc(xs_rdy, 1)
                dve.wait_ge(xa_rdy, 2 * g + 2)
                nc.vector.tensor_tensor(xl[:, ct], xf[:, 0, ct], xh[:, ct].bitcast(F32), ALU.subtract).then_inc(xs_rdy, 1)

            dve.wait_ge(d_misc, 32)
            nc.vector.tensor_copy(selr[:], sel_s[:]).then_inc(zeroed, 1)
            def zt_src(t, r):
                return zt[r, t, :]

            dve.wait_ge(tok_mm, 1)
            first_half(0)
            first_scale(0, 1)
            norm_stats(zt_src, full[:2])
            dve.wait_ge(tok_mm, 2)
            first_half(1)
            second_scale(0, 2)
            first_scale(1, 3)
            norm_stats(zt_src, full[2:])
            split_tokens(0)
            second_scale(1, 4)
            split_tokens(1)

            def routed(i, sl):
                dve.wait_ge(h_read, i * 2 * FK + (sl + 3))
                if sl >= 2:
                    dve.wait_ge(hl_rdy, i * 2 * FK + sl)
                nc.vector.tensor_tensor(hw[:, sl % 2, :], hg[:, sl % 2, :], cb[:, bass.ds(i * 2 + sl // FK, 1), :],
                                        ALU.mult).then_inc(hw_rdy, 1)

            dve.wait_ge(lg_mm, 1)
            own(nc.vector.tensor_tensor(lg[:], lg_ps[:, :, 0:E],
                                        rowb[:, 2 * D:2 * D + E].unsqueeze(1).to_broadcast([P, NT, E]), ALU.add))
            nc.vector.tensor_tensor(vt[:], lg_ps[:, :, E:E + 1].to_broadcast([P, NT, P // HB]),
                                    blk_s.unsqueeze(1).to_broadcast([P, NT, P // HB]), ALU.mult).then_inc(vt_rdy, 1)
            dve.wait_ge(v_done, n)
            cand = lg[:].unsqueeze(2).to_broadcast([P, NT, E, E])
            for e in range(E):
                me = lg[:, :, e:e + 1]
                if e:
                    own(nc.vector.tensor_tensor(lgt[:, :, e, 0:e], lg[:, :, 0:e], me.to_broadcast([P, NT, e]),
                                                ALU.is_ge))
                own(nc.vector.tensor_tensor(lgt[:, :, e, e:E], lg[:, :, e:E], me.to_broadcast([P, NT, E - e]),
                                            ALU.is_gt))
            own(nc.vector.tensor_reduce(sc[:, 0, :], lg[:], AX.X, ALU.max))
            dve.wait_ge(v_done, n)
            own(nc.vector.tensor_reduce(rk[:], lgt[:], AX.X, ALU.add))
            nc.vector.tensor_tensor(lg[:], lg[:], sc[:, 0, :].unsqueeze(2).to_broadcast([P, NT, E]),
                                    ALU.subtract).then_inc(lg_max, 1)
            dve.wait_ge(d_ffn, 96)
            for f in range(2):
                r = slice(32 * f, 32 * f + B)
                nc.vector.tensor_tensor(ow[r, 0:D], ow[r, 0:D], bkr[r, :], ALU.mult).then_inc(ow_rdy, 1)
            dve.wait_ge(v_done, n)
            dve.wait_ge(lg_exp, 1)
            link(nc.vector.scalar_tensor_tensor(out=comb[:], in0=rk[:], scalar=1.5, in1=comb[:],
                                                op0=ALU.is_lt, op1=ALU.mult))
            link(nc.vector.tensor_reduce(sc[:, 1, :], comb[:], AX.X, ALU.add))
            link(nc.vector.reciprocal(sc[:, 2, :], sc[:, 1, :]))
            link(nc.vector.tensor_tensor(comb[:], comb[:], sc[:, 2, :].unsqueeze(2).to_broadcast([P, NT, E]), ALU.mult))
            link(nc.vector.tensor_copy(comb2[:, :, 0:E], comb[:]))
            nc.vector.tensor_tensor(comb2[:, :, E:], comb[:], comb2[:, :, 0:E].bitcast(F32),
                                    ALU.subtract).then_inc(comb_rdy, 1)
            dve.wait_ge(hi1, 2)
            split_lo1(1)
            dve.wait_ge(combt_mm, 1)
            nc.vector.tensor_copy(combt[:], combt_ps).then_inc(combt_rdy, 1)
            dve.wait_ge(v_mm, 1)
            for r, order in ((slice(0, 32), slice(None)), (slice(32, 64), slice(None, None, -1))):
                nc.vector.tensor_scalar(vseq[r, order], v_ps[r, :], vcol("v_b", 0, r), 3.0, ALU.add,
                                        ALU.min).then_inc(v_ev, 1)
            for e in range(1, E, 2):
                for h in range(2):
                    dve.wait_ge(cb_mm, 2 * e + h + 1)
                    nc.vector.tensor_copy(cb[:, e, h * FH:(h + 1) * FH], ps[:, 6 + h, 0:FH]).then_inc(cb_odd, 1)
                if e == 1:
                    dve.wait_ge(v_ev, 2)
                    link(nc.vector.tensor_scalar(vseq[:], vseq[:], -3.0, -2.0, ALU.max, ALU.add))
                if e == 3:
                    nc.vector.tensor_copy(ar[:, :, 1], vseq[:]).then_inc(vseq_rdy, 1)
                    nc.vector.tensor_scalar(ar[:, :, 0], vseq[:], -1.0, None, ALU.mult).then_inc(vseq_rdy, 1)
                if e == 3:
                    dve.wait_ge(cb_even, 2)
                    routed(0, 0)
            routed(0, 1)
            dve.sem_inc(hl_rdy, 1)
            dve.wait_ge(cb_odd, E)
            dve.wait_ge(cb_even, E)

            def pair_of_experts(i, last):
                for sl in range(2 * FK):
                    j, k = divmod(sl, FK)
                    s = i * 2 * FK + sl
                    dve.wait_ge(hh_rdy, s + 1)
                    nc.vector.tensor_tensor(hl[:, sl % RING, :], hw[:, sl % 2, :], hh[:, sl % RING, :].bitcast(F32),
                                            ALU.subtract).then_inc(hl_rdy, 1)
                    if not (last and sl >= 2 * FK - 2):
                        routed(i, sl + 2)
                    if k in (K_HI2 + 1, K_HI2 + 2) and not (last and j == 1):
                        dve.wait_ge(hi2, i * 2 + (j + 2))
                        split_lo2(1 - j, k - K_HI2 - 1)
                    if k == K_HI1 + 1 and not last:
                        dve.wait_ge(hi1, i * 2 + (j + 3))
                        split_lo1(j)

            with dve.Fori(0, E // 2 - 1) as i:
                pair_of_experts(i, False)
            pair_of_experts(E // 2 - 1, True)

            q = NT - 1

            def residual(tiles):
                for t, r in tiles:
                    bank, off = (0, 2)[t // 2 % 2] + t // 4, (t % 2) * D
                    if t in (0, 2, q):
                        dve.wait_ge(yt_mm, t // 2 + 1)
                    own(nc.vector.tensor_tensor(zt[r, t, :], ps[r, bank, off:off + D], ht[r, t, 0:D], ALU.add))
                dve.wait_ge(v_done, n)

            def last_norm(tiles, k):
                dve.wait_ge(rstd_rdy, k)
                for t, r in tiles:
                    nc.vector.tensor_scalar(zt[r, t, :], zt[r, t, :], mv[r, t, 0:1], rstd[r, t:t + 1],
                                            ALU.subtract, ALU.mult).then_inc(fin_rdy, 1)

            for h in range(2):
                dve.wait_ge(y_mm, h + 1)
                c = slice(h * FH, min((h + 1) * FH, NPX))
                nc.vector.tensor_scalar(yt[:, 1, c], ps[:, 6 + h, 0:c.stop - c.start], gate[:, 5:6], None,
                                        ALU.add).then_inc(y_evb, 1)
            nc.vector.tensor_scalar(ycls[:, 1:2], ps[:, 7, NPX - FH:NPX - FH + 1], gate[:, 5:6], None,
                                    ALU.add).then_inc(y_evb, 1)
            dve.wait_ge(y_evb, 3)
            nc.vector.tensor_scalar(yt[:, 1, NPX:TOK], ps[:, 7, FH:FH + B], ycls[:, 1:2], None,
                                    ALU.add).then_inc(y_evb, 1)
            residual(full[:2])
            norm_stats(zt_src, full[:2])
            residual(full[2:q] + [(q, slice(0, TOK - q * P))])
            norm_stats(zt_src, full[2:])
            last_norm(full[:2], 5)
            last_norm(full[2:], 6)

        @block.tensor
        def _(pe):
            mm = nc.tensor.matmul
            pe.wait_ge(d_had, 32)
            for pt in range(2):
                b = 4 + 2 * pt
                for bank, cs in ((b, slice(0, 2 * D)), (b + 1, slice(2 * D, 3 * D))):
                    for k in range(2):
                        last = mm(ps[:, bank, 0:cs.stop - cs.start], had_s[:, k, pt * P:(pt + 1) * P],
                                  w1t_s[:, k, cs], start=(k == 0), stop=(k == 1))
                last.then_inc(had_mm, 1)

            def embed_half(g):
                for m in range(3):
                    for k in range(KT):
                        if m == 0:
                            pe.wait_ge(d_x[2 * g + k // (KT // 2)], 16)
                        if m == 1 and k == 0 and g == 0:
                            pe.wait_ge(had_cp, 4)
                        last = mm(ps[:, 4 * g + m, 0:HPX], embed[:, k, m * P:(m + 1) * P],
                                  x_s[:, k, g * HPX:(g + 1) * HPX], start=(k == 0), stop=(k == KT - 1))
                    last.then_inc(emb_mm, 1)

            def pointwise(conv_, src, g, bank, kb, ka_tile, m, orows):
                c = slice(g * HPX, (g + 1) * HPX)
                mm(ps[orows, bank, 0:HPX], pw_s[:, conv_, 0, m], src[:, ka_tile, c], start=True, stop=False)
                mm(ps[orows, bank, 0:HPX], pw_s[kb, conv_, 1, m], src[kb, 1, c],
                   start=False, stop=True).then_inc(pw_mm, 1)

            MA, MB = slice(0, P), slice(P, D)

            def branches(g):
                b = 4 * g
                pe.wait_ge(dw_done, 3 * g + 3)
                pointwise(1, act_b, g, b + 2, HI, 2, MA, A)
                pointwise(1, act_b, g, b + 1, HI, 2, MB, HI)
                pointwise(0, act_b, g, b, LO, 0, MA, A)
                pointwise(0, act_b, g, b + 1, LO, 0, MB, LO)
                pe.wait_ge(pw_ev, 6 * g + 2)
                if g == 0:
                    pe.wait_ge(attn_rdy, 1)
                pointwise(2, loc, g, b + 2, HI, 2, MA, A)
                pointwise(2, loc, g, b + 3, HI, 2, MB, LO)

            def fusion(f, g):
                b = 4 * g
                src = act_b
                pe.wait_ge(dw_done, 6 + 4 * f + 2 * g + 2)
                pointwise(3 + f, src, g, b, LO, 0, MA, A)
                pointwise(3 + f, src, g, b + 1, LO, 0, MB, LO)

            def taps(f, g):
                if f == 0:
                    pe.wait_ge(mixed, 2 * g + 2)
                elif f == 1:
                    pe.wait_ge(pw_ev, 12 + 2 * g + 2)
                else:
                    pe.wait_ge(mixed, 4 + 2 * g + 2)
                pe.wait_ge(diag_rdy, 6 * (f + 1))
                for t, rows_ in ((0, A), (1, LO)):
                    tap_sums((act_a, act_a, glob)[f], g, t, rows_, diag[:, f, t], 4 * g + 2 + t)

            def tap_sums(src, g, t, rows_, mats, bank):
                v = src[rows_, t, g * HPX:(g + 1) * HPX].rearrange("p (y x) -> p y x", y=G)
                o = ps[rows_, bank, 0:HPX].rearrange("p (y x) -> p y x", y=G)
                for m, (dy, dx) in enumerate(PE_TAPS):
                    x0, x1 = max(0, -dx), G - max(0, dx)
                    last = mm(o[:, 1:G, x0 * HB:x1 * HB], mats[rows_, m, 0:rows_.stop],
                              v[:, 0:G - 1, (x0 + dx) * HB:(x1 + dx) * HB],
                              start=(m == 0), stop=(m == len(PE_TAPS) - 1))
                last.then_inc(tap_mm, 1)

            pe.wait_ge(d_plw, 16)
            embed_half(0)
            embed_half(1)
            pe.wait_ge(d_proj, 32)
            pe.wait_ge(zeroed, 3)
            mm(ps[:, 3, 0:D], zero[:], proj_s[:, 0, :], start=True, stop=False)
            mm(ps[:, 3, 0:D], zero[LO, :], proj_s[LO, 1, :], start=False, stop=False)
            mm(ps[:, 3, 0:D], ones[:], projb_s[:], start=False, stop=True).then_inc(attn_mm, 1)
            pe.wait_ge(d_pw, 16)
            branches(0)
            branches(1)
            for f in range(3):
                for g in range(2):
                    if (f, g) in PE_HELPS:
                        taps(f, g)
                    fusion(f, g)
            for group, done in (((0, 1), 22), ((2, 3, 4), 24)):
                pe.wait_ge(pw_ev, done)
                if group[0] == 0:
                    pe.wait_ge(d_misc, 32)
                for t in group:
                    c = slice(t * P, min((t + 1) * P, NPX))
                    w = c.stop - c.start
                    nc.tensor.transpose(tok_ps[t][0:w, 0:P], act_a[:, 0, c], id_s[:])
                    last = nc.tensor.transpose(tok_ps[t][0:w, P:D], act_a[LO, 1, c], id_s[LO, 0:DB])
                last.then_inc(tok_mm, 1)
            for g, tiles in enumerate(groups):
                for k, t in enumerate(tiles):
                    pe.wait_ge(ht_rdy, t + 1)
                    last = nc.tensor.transpose(xa_ps[g][:, k * P:(k + 1) * P], ht[:, t, 0:P], id_s[:])
                last.then_inc(xt_mm, 1)
                for k, t in enumerate(tiles):
                    last = nc.tensor.transpose(xb_ps[g][LO, k * P:(k + 1) * P], ht[:, t, P:D], id_s[:])
                last.then_inc(xt_mm, 1)
                for k, t in enumerate(tiles):
                    last = nc.tensor.transpose(xc_ps[g][:, k * P:(k + 1) * P], ht[:, t, DB:D], id_s[:])
                last.then_inc(xt_mm, 1)
                pe.wait_ge(xa_rdy, 2 * g + 1)
                pe.wait_ge(xf_rdy, g + 1)
                for t in tiles:
                    c = slice(t * P, (t + 1) * P)
                    gw = V["gate_w"]
                    mm(lg_ps[:, t, :], xf[:, 0, c], vecs[:, gw:gw + E + 1], start=True, stop=False)
                    last = mm(lg_ps[:, t, :], xf[LO, 1, c], vecs[LO, gw + E + 1:gw + 2 * E + 2],
                              start=False, stop=True)
            last.then_inc(lg_mm, 1)
            pe.sem_inc(l2_mm, RING)

            def first_product_half(slot, k, hs, h):
                f = slice(k * P, (k + 1) * P)
                c = slice(h * FH, (h + 1) * FH)
                o = ps[:, 2 * hs + h, 0:FH]
                mm(o, w1h[:, slot, 0, f], xh[:, c], start=True, stop=False)
                mm(o, w1h[:, slot, 0, f], xl[:, c], start=False, stop=False)
                mm(o, w1l[:, slot, 0, f], xh[:, c], start=False, stop=False)
                mm(o, w1h[:, slot, 1, f], xb[:, c], start=False, stop=False)
                return mm(o, w1l[LO, slot, 1, f], xb[LO, c], start=False, stop=True)

            def first_product(slot, k, hs):
                first_product_half(slot, k, hs, 0)
                return first_product_half(slot, k, hs, 1)

            def second_product(slot, k, r):
                for h in range(2):
                    c = slice(h * FH, (h + 1) * FH)
                    oa, ob = ps[:, 4 + h, 0:FH], ps[:, 6 + h, 0:FH]
                    mm(oa, w2s[:, slot, k, 0:P], hh[:, r, c], start=False, stop=False)
                    mm(oa, w2s[:, slot, k, 256:384], hh[:, r, c], start=False, stop=False)
                    mm(ob, w2s[:, slot, k, P:256], hh[:, r, c], start=False, stop=False)
                    mm(oa, w2s[:, slot, k, 0:P], hl[:, r, c], start=False, stop=False)
                    last = mm(ps[LO, 6 + h, 0:FH], w2s[:, slot, k, P:D], hl[:, r, c], start=False, stop=False)
                return last

            pe.wait_ge(xs_rdy, 6)
            pe.wait_ge(lo1, 1)
            first_product(0, 0, 0).then_inc(l1_mm, 1)
            first_product(0, 1, 1).then_inc(l1_mm, 1)
            pe.wait_ge(vt_rdy, 1)
            vcols = vt[:].rearrange("p t j -> p (t j)")
            for o, c0, w in ((1, 0, SEQ - 1), (0, NPX // HB, 1)):
                for g in range(2):
                    last = mm(v_ps[:, o:o + w], img_s[:, g, :], vcols[:, c0 + g * w:c0 + (g + 1) * w],
                              start=(g == 0), stop=(g == 1))
            last.then_inc(v_mm, 1)
            pe.wait_ge(comb_rdy, 1)
            for t in range(NT):
                last = nc.tensor.transpose(combt_ps[:, t * P:(t + 1) * P], comb2[:, t, :].bitcast(F32), id_s[:])
            last.then_inc(combt_mm, 1)
            pe.wait_ge(h_read, 3)
            first_product(0, 2, 0).then_inc(l1_mm, 1)
            pe.wait_ge(combt_rdy, 1)
            pe.wait_ge(zeroed, 4)
            for e in range(E):
                if e in (3, 6):
                    pe.wait_ge(h_read, 4)
                    last = first_product_half(0, 3, 1, e // 6)
                    if e == 6:
                        last.then_inc(l1_mm, 1)
                for h in range(2):
                    if e == 1 and h == 1:
                        pe.wait_ge(v_ev, 2)
                    if e >= 2:
                        pe.wait_ge(cb_odd if e % 2 else cb_even, 2 * (e // 2 - 1) + h + 1)
                    mm(ps[:, 4 + 2 * (e % 2) + h, 0:FH], selr[:, e * P:(e + 1) * P],
                       combt[:, h * FH:(h + 1) * FH], start=True, stop=True).then_inc(cb_mm, 1)
            for b in range(4, 8):
                pe.wait_ge(cb_even if b < 6 else cb_odd, E)
                mm(ps[:, b, 0:FH], zeror[:], combt[:, 0:FH], start=True, stop=False)
            def pair_of_experts(i, last):
                for sl in range(2 * FK):
                    j, k = divmod(sl, FK)
                    s = i * 2 * FK + sl
                    if k == 0:
                        pe.wait_ge(lo2, i * 4 + 2 * (j + 1))
                    pe.wait_ge(hl_rdy, s + 2)
                    second_product(j, k, sl % RING).then_inc(l2_mm, 1)
                    if last and sl + LAG >= 2 * FK:
                        continue
                    j1, k1 = divmod(sl + LAG, FK)
                    if k1 == 0:
                        pe.wait_ge(lo1, i * 2 + (j1 + 1))
                    pe.wait_ge(h_read, s + (LAG + 1))
                    first_product(j1 % 2, k1, sl % 2).then_inc(l1_mm, 1)

            with pe.Fori(0, E // 2 - 1) as i:
                pair_of_experts(i, False)
            pair_of_experts(E // 2 - 1, True)
            pe.wait_ge(bk_rdy, 8)
            pe.wait_ge(ow_rdy, 2)
            for h in range(2):
                c = slice(h * FH, (h + 1) * FH)
                mm(ps[:, 4 + h, 0:FH], ow[:, 0:P], gm[:, c], start=False, stop=True)
                last = mm(ps[:, 6 + h, 0:FH], ow[:, P:2 * P], gm[:, c], start=False, stop=True)
                if h:
                    mm(ps[:, 5, FH:FH + B], ow[:, 0:P], gm[:, FT:], start=True, stop=True)
                    last = mm(ps[:, 7, FH:FH + B], ow[:, P:2 * P], gm[:, FT:], start=True, stop=True)
                last.then_inc(y_mm, 1)
            for t in range(NT):
                if t in (0, 2, NT - 1):
                    pe.wait_ge(y_ev, (1, 2, 4)[t // 2])
                    pe.wait_ge(y_evb, (1, 2, 4)[t // 2])
                c = slice(t * P, min((t + 1) * P, TOK))
                w = c.stop - c.start
                bank, off = (0, 2)[t // 2 % 2] + t // 4, (t % 2) * D
                nc.tensor.transpose(ps[0:w, bank, off:off + P], yt[:, 0, c], id_s[:])
                last = mm(ps[0:w, bank, off + P:off + D], yt[:, 1, c], pair_s, start=True, stop=True)
                if t % 2 or t == NT - 1:
                    last.then_inc(yt_mm, 1)


def haar_matrix():
    k = np.arange(256)[:, None]
    px = np.arange(256)[None, :]
    r, c = px // 16, px % 16
    s = np.zeros((256, 256), np.int64)
    for lv in range(4):
        band = (k >> (2 * (3 - lv))) & 3
        s += (band >> 1) * ((c >> lv) & 1) + (band & 1) * ((r >> lv) & 1)
    return np.where(s % 2, -0.0625, 0.0625).astype(np.float32)


def kernel(**inputs):
    import concourse.bacc as bacc
    from concourse.bass_utils import run_bass_kernel_spmd

    t = {k.replace("L0_tok_", "").replace("L0_attn_", "").replace("L0_ffn_", "f_"): np.asarray(v)
         for k, v in inputs.items()}
    f32 = np.float32

    def parts(v):
        v = v.reshape(D, -1)
        o = np.zeros((P, 2, v.shape[1]), f32)
        o[:, 0] = v[:P]
        o[:DB, 1] = v[P:]
        return o

    def three(a, g):
        a, g = a.reshape(D, -1), g.reshape(D, -1)
        return np.stack([a[:P], np.concatenate([a[P:], g[P:]]), g[:P]], 1)

    vec = np.zeros((P, NVEC), f32)

    def put(name, v):
        v = v.reshape(P, -1)
        vec[:, V[name]:V[name] + v.shape[1]] = v

    put("dw1", three(t["pl_dw"], t["pg_dw"]))
    put("dwf", np.stack([parts(t[f"f{i}_dw"]) for i in (1, 2, 3)], 1))
    put("bias1", three(t["pl_b"], t["pg_b1"]))
    put("bias2", three(t["pl_pwb"], t["pg_pwb"]))
    put("b_w2", parts(t["pg_b2"]))
    put("alpha", parts(t["alpha"]))
    put("fb", np.stack([parts(t[f"f{i}_pwb"]) for i in (1, 2, 3)], 1))
    put("bk", parts(t["f_bk_scale"]))
    put("out_b", parts(t["f_out_b"]))
    put("gate_w", parts(np.concatenate([t["f_gate_w"].reshape(D, E), t["f_v_w"].reshape(D, 1)], 1)))
    put("v_b", np.broadcast_to(t["f_v_b"].reshape(1, 1), (P, 1)))
    put("b1", t["f_b1"].reshape(E, FK, P).transpose(2, 0, 1))

    x = t["x"].reshape(2, HB, CIN, G, PATCH, G, PATCH).transpose(0, 2, 4, 6, 3, 5, 1)
    x = x.reshape(2, KT, P, HPX).transpose(0, 2, 1, 3)
    plw = t["pl_w"].reshape(D, KP).T.reshape(KT, P, D).transpose(1, 0, 2)
    w1t = t["pg_w1"].reshape(D, 256, CIN)
    w1t = np.concatenate([w1t[P:], w1t[:P]]).transpose(1, 2, 0).reshape(2, P, CIN * D).transpose(1, 0, 2)
    had = haar_matrix().reshape(2, P, 256).transpose(1, 0, 2)
    pw = np.zeros((P, 6, 2, D), f32)
    for i, (name, rows) in enumerate([("pl_pw", 0), ("pg_pw", DB), ("pg_w2", DB), ("f1_pw", 0), ("f2_pw", 0),
                                      ("f3_pw", 0)]):
        w = t[name].reshape(D, D).T
        pw[:, i, 0] = w[:P]
        pw[rows:rows + DB, i, 1] = w[P:]
    projw = np.zeros((P, 3 * D), f32)
    projw[:, :2 * D] = parts(t["proj_w"].T).reshape(P, 2 * D)
    projw[0, 2 * D:] = t["proj_b"]
    rows = np.concatenate([t["ln_g"], t["ln_b"], t["f_gate_b"], t["f_bk_scale"]]).reshape(1, -1)
    ident = np.eye(P, dtype=f32)
    rr = np.arange(P)
    img = np.zeros((P, 2, DB), f32)
    for g in range(2):
        for o in (0, 32):
            img[rr, g, o + HB * g + rr % HB] = 1.0
    layout = np.concatenate([np.tile(np.eye(DB, dtype=f32), (2, 1)), np.repeat(np.eye(P // HB, dtype=f32), HB, 0),
                             img.reshape(P, 2 * DB)], 1)
    sel = np.zeros((2, E, E, P), f32)
    for e in range(E):
        sel[:, e, e] = 1.0
    arrays = {
        "x": x, "vec": vec, "rows": rows, "had": had, "w1t": w1t, "plw": plw, "pw": pw, "projw": projw,
        "cls": t["cls"].reshape(1, D), "ident": ident, "layout": layout, "sel": sel.reshape(2 * E, E * P),
        "w1": t["f_w1"], "w2": t["f_w2"].reshape(E, FK, P, D).transpose(0, 2, 1, 3), "b2": t["f_b2"],
        "outw": t["f_out_w"],
    }
    nc = bacc.Bacc("TRN2", target_bir_lowering=False, num_devices=1)
    arrays = {k: np.ascontiguousarray(v) for k, v in arrays.items()}
    args = {k: nc.dram_tensor("in_" + k, v.shape, mybir.dt.from_np(v.dtype), kind="ExternalInput").ap()
            for k, v in arrays.items()}
    out = nc.dram_tensor("out_tokens", (TOK, D), F32, kind="ExternalOutput").ap()
    tower(nc, out=out, **args)
    r = run_bass_kernel_spmd(nc, [{"in_" + k: v for k, v in arrays.items()}], core_ids=[0])
    got = np.asarray(r.results[0]["out_tokens"])
    px = got[:NPX].reshape(2, G * G, HB, D).transpose(0, 2, 1, 3).reshape(B, G * G, D)
    return np.concatenate([got[NPX:][:, None], px], axis=1)
```
